# Optimizing a Trainium2 kernel written in Bass

```python
import numpy as np
import jax
import jax.numpy as jnp

def _softmax(x, axis=-1):
    return jax.nn.softmax(x, axis=axis)

def _gelu(x):
    return jax.nn.gelu(x, approximate=True)

def _silu(x):
    return jax.nn.silu(x)

def _sigmoid(x):
    return jax.nn.sigmoid(x)

def _layernorm(x, axis=-1, eps=1e-05):
    m = jnp.mean(x, axis=axis, keepdims=True)
    v = jnp.var(x, axis=axis, keepdims=True)
    return (x - m) / jnp.sqrt(v + eps)

def _scatter_add(tgt, idx, src, axis=0):
    return tgt.at[idx].add(src)

def _segment_sum(src, seg, n):
    return jax.ops.segment_sum(src, seg, n)
kernel_name = 'mk_seq_postln_d1_jaxref_r4_17ef04'

def setup_inputs(seed: int=0):
    np.random.seed(seed)
    _w = jnp.asarray

    def _L0_attn_setup():
        import jax, jax.numpy as jnp
        import numpy as np
        from jax import lax
        SHIFT = 1
        GAMMA = 0.25

        def q_shift_1d(x, shift=SHIFT, gamma=GAMMA):
            B, T, C = x.shape
            c1 = int(C * gamma)
            c2 = int(C * gamma * 2)
            fwd = jnp.pad(x[:, :T - shift, :c1], ((0, 0), (shift, 0), (0, 0)))
            bwd = jnp.pad(x[:, shift:, c1:c2], ((0, 0), (0, shift), (0, 0)))
            return jnp.concatenate([fwd, bwd, x[:, :, c2:]], axis=-1)

        def wkv_scan(w, u, k, v):
            B, T, C = k.shape
            ew = jnp.exp(w)

            def step(carry, kv):
                a, b = carry
                kt, vt = kv
                eku = jnp.exp(u + kt)
                out = (a + eku * vt) / (b + eku)
                ek = jnp.exp(kt)
                return ((a * ew + ek * vt, b * ew + ek), out)
            k_t = jnp.moveaxis(k, 1, 0)
            v_t = jnp.moveaxis(v, 1, 0)
            init = (jnp.zeros((B, C), k.dtype), jnp.zeros((B, C), k.dtype))
            _, ys = lax.scan(step, init, (k_t, v_t))
            return jnp.moveaxis(ys, 0, 1)
        key = jax.random.key(seed)
        ks = jax.random.split(key, 10)
        B, T, C = (8, 1024, 256)
        s = 1.0 / np.sqrt(C)
        return {'x': jax.random.normal(ks[0], (B, T, C), jnp.float32), 'Wk': jax.random.normal(ks[1], (C, C), jnp.float32) * s, 'Wv': jax.random.normal(ks[2], (C, C), jnp.float32) * s, 'Wr': jax.random.normal(ks[3], (C, C), jnp.float32) * s, 'Wo': jax.random.normal(ks[4], (C, C), jnp.float32) * s, 'spatial_decay': jax.random.normal(ks[5], (C,), jnp.float32), 'spatial_first': jax.random.normal(ks[6], (C,), jnp.float32), 'mix_k': jax.random.uniform(ks[7], (C,), jnp.float32), 'mix_v': jax.random.uniform(ks[8], (C,), jnp.float32), 'mix_r': jax.random.uniform(ks[9], (C,), jnp.float32)}
    _L0_attn_in = _L0_attn_setup()

    def _L0_ffn_setup():
        import jax, jax.numpy as jnp
        import numpy as np
        B, S, D, H, F = (4, 1024, 256, 16, 1024)
        CAP = 0.125
        ROPE_BASE = 10000.0

        def rmsnorm(x, g):
            return x * jax.lax.rsqrt(jnp.mean(x * x, -1, keepdims=True) + 1e-06) * g

        def rope(t, pos):
            hd = t.shape[-1]
            inv = 1.0 / ROPE_BASE ** (jnp.arange(0, hd, 2, dtype=jnp.float32) / hd)
            f = pos[:, None, :, None].astype(jnp.float32) * inv
            emb = jnp.concatenate([f, f], axis=-1)
            cos, sin = (jnp.cos(emb), jnp.sin(emb))
            rot = jnp.concatenate([-t[..., hd // 2:], t[..., :hd // 2]], axis=-1)
            return t * cos + rot * sin
        key = jax.random.key(seed)
        ks = jax.random.split(key, 9)
        scale = 0.02
        x = jax.random.normal(ks[0], (B, S, D), jnp.float32)
        causal = jnp.where(jnp.tril(jnp.ones((S, S), bool)), 0.0, -1000000000.0).astype(jnp.float32)
        attention_mask = jnp.broadcast_to(causal[None, None], (B, 1, S, S))
        position_ids = jnp.broadcast_to(jnp.arange(S, dtype=jnp.int32), (B, S))
        return {'x': x, 'attention_mask': attention_mask, 'position_ids': position_ids, 'router_w': jax.random.normal(ks[1], (D, 1), jnp.float32) * scale, 'router_b': jnp.zeros((1,), jnp.float32), 'wq': jax.random.normal(ks[2], (D, D), jnp.float32) * scale, 'wk': jax.random.normal(ks[3], (D, D), jnp.float32) * scale, 'wv': jax.random.normal(ks[4], (D, D), jnp.float32) * scale, 'wo': jax.random.normal(ks[5], (D, D), jnp.float32) * scale, 'w1': jax.random.normal(ks[6], (D, F), jnp.float32) * scale, 'w2': jax.random.normal(ks[7], (F, D), jnp.float32) * scale, 'ln1': jnp.ones((D,), jnp.float32), 'ln2': jnp.ones((D,), jnp.float32)}
    _L0_ffn_in = _L0_ffn_setup()
    _d = {'L0_attn_x': _L0_attn_in['x'], 'L0_attn_Wk': _L0_attn_in['Wk'], 'L0_attn_Wv': _L0_attn_in['Wv'], 'L0_attn_Wr': _L0_attn_in['Wr'], 'L0_attn_Wo': _L0_attn_in['Wo'], 'L0_attn_spatial_decay': _L0_attn_in['spatial_decay'], 'L0_attn_spatial_first': _L0_attn_in['spatial_first'], 'L0_attn_mix_k': _L0_attn_in['mix_k'], 'L0_attn_mix_v': _L0_attn_in['mix_v'], 'L0_attn_mix_r': _L0_attn_in['mix_r'], 'L0_ffn_attention_mask': _L0_ffn_in['attention_mask'], 'L0_ffn_position_ids': _L0_ffn_in['position_ids'], 'L0_ffn_router_w': _L0_ffn_in['router_w'], 'L0_ffn_router_b': _L0_ffn_in['router_b'], 'L0_ffn_wq': _L0_ffn_in['wq'], 'L0_ffn_wk': _L0_ffn_in['wk'], 'L0_ffn_wv': _L0_ffn_in['wv'], 'L0_ffn_wo': _L0_ffn_in['wo'], 'L0_ffn_w1': _L0_ffn_in['w1'], 'L0_ffn_w2': _L0_ffn_in['w2'], 'L0_ffn_ln1': _L0_ffn_in['ln1'], 'L0_ffn_ln2': _L0_ffn_in['ln2']}
    _x0 = _d['L0_attn_x']
    _d['L0_attn_x'] = jax.random.normal(jax.random.fold_in(jax.random.key(seed), 1), (32, 512, 256), dtype=_x0.dtype)
    del _x0
    return _d

def reference(L0_attn_x, L0_attn_Wk, L0_attn_Wv, L0_attn_Wr, L0_attn_Wo, L0_attn_spatial_decay, L0_attn_spatial_first, L0_attn_mix_k, L0_attn_mix_v, L0_attn_mix_r, L0_ffn_attention_mask, L0_ffn_position_ids, L0_ffn_router_w, L0_ffn_router_b, L0_ffn_wq, L0_ffn_wk, L0_ffn_wv, L0_ffn_wo, L0_ffn_w1, L0_ffn_w2, L0_ffn_ln1, L0_ffn_ln2):

    def _L0_attn_ref(x, Wk, Wv, Wr, Wo, spatial_decay, spatial_first, mix_k, mix_v, mix_r):
        import jax, jax.numpy as jnp
        import numpy as np
        from jax import lax
        SHIFT = 1
        GAMMA = 0.25

        def q_shift_1d(x, shift=SHIFT, gamma=GAMMA):
            B, T, C = x.shape
            c1 = int(C * gamma)
            c2 = int(C * gamma * 2)
            fwd = jnp.pad(x[:, :T - shift, :c1], ((0, 0), (shift, 0), (0, 0)))
            bwd = jnp.pad(x[:, shift:, c1:c2], ((0, 0), (0, shift), (0, 0)))
            return jnp.concatenate([fwd, bwd, x[:, :, c2:]], axis=-1)

        def wkv_scan(w, u, k, v):
            B, T, C = k.shape
            ew = jnp.exp(w)

            def step(carry, kv):
                a, b = carry
                kt, vt = kv
                eku = jnp.exp(u + kt)
                out = (a + eku * vt) / (b + eku)
                ek = jnp.exp(kt)
                return ((a * ew + ek * vt, b * ew + ek), out)
            k_t = jnp.moveaxis(k, 1, 0)
            v_t = jnp.moveaxis(v, 1, 0)
            init = (jnp.zeros((B, C), k.dtype), jnp.zeros((B, C), k.dtype))
            _, ys = lax.scan(step, init, (k_t, v_t))
            return jnp.moveaxis(ys, 0, 1)
        B, T, C = x.shape
        xx = q_shift_1d(x)
        xk = x * mix_k + xx * (1.0 - mix_k)
        xv = x * mix_v + xx * (1.0 - mix_v)
        xr = x * mix_r + xx * (1.0 - mix_r)
        k = jnp.einsum('btc,oc->bto', xk, Wk)
        v = jnp.einsum('btc,oc->bto', xv, Wv)
        r = jnp.einsum('btc,oc->bto', xr, Wr)
        sr = jax.nn.sigmoid(r)
        wkv_out = wkv_scan(spatial_decay / T, spatial_first / T, k, v)
        return jnp.einsum('btc,oc->bto', sr * wkv_out, Wo)

    def _L0_ffn_ref(x, attention_mask, position_ids, router_w, router_b, wq, wk, wv, wo, w1, w2, ln1, ln2):
        import jax, jax.numpy as jnp
        import numpy as np
        B, S, D, H, F = (4, 1024, 256, 16, 1024)
        CAP = 0.125
        ROPE_BASE = 10000.0

        def rmsnorm(x, g):
            return x * jax.lax.rsqrt(jnp.mean(x * x, -1, keepdims=True) + 1e-06) * g

        def rope(t, pos):
            hd = t.shape[-1]
            inv = 1.0 / ROPE_BASE ** (jnp.arange(0, hd, 2, dtype=jnp.float32) / hd)
            f = pos[:, None, :, None].astype(jnp.float32) * inv
            emb = jnp.concatenate([f, f], axis=-1)
            cos, sin = (jnp.cos(emb), jnp.sin(emb))
            rot = jnp.concatenate([-t[..., hd // 2:], t[..., :hd // 2]], axis=-1)
            return t * cos + rot * sin
        b, s, d = x.shape
        hd = d // H
        weights = (x @ router_w)[..., 0] + router_b[0]
        k = int(CAP * s)
        topv, topi = jax.lax.top_k(weights, k)
        thr = topv[:, -1]
        sel_mask = (weights > thr[:, None]).astype(x.dtype)
        kc = k - 1
        sel_idx = jnp.sort(topi[:, :kc], axis=1)
        bidx = jnp.arange(b)[:, None]
        x_sel = x[bidx, sel_idx]
        pos_sel = position_ids[bidx, sel_idx]
        w_sel = weights[bidx, sel_idx]
        m = attention_mask[:, 0]
        m_sel = m[bidx[:, :, None], sel_idx[:, :, None], sel_idx[:, None, :]]
        hn = rmsnorm(x_sel, ln1)

        def heads(t):
            return t.reshape(b, kc, H, hd).transpose(0, 2, 1, 3)
        q = rope(heads(hn @ wq), pos_sel)
        kk = rope(heads(hn @ wk), pos_sel)
        v = heads(hn @ wv)
        sc = jnp.einsum('bhqd,bhkd->bhqk', q, kk) / np.sqrt(hd).astype(np.float32)
        sc = sc + m_sel[:, None]
        a = jax.nn.softmax(sc, axis=-1)
        o = jnp.einsum('bhqk,bhkd->bhqd', a, v).transpose(0, 2, 1, 3).reshape(b, kc, d) @ wo
        x1 = x_sel + o
        x2 = x1 + jax.nn.gelu(rmsnorm(x1, ln2) @ w1) @ w2
        proc = x2 * w_sel[..., None]
        out = jnp.zeros_like(x).at[bidx, sel_idx].set(proc)
        return out + x * (1.0 - sel_mask)[..., None]
    x = L0_attn_x
    x = _layernorm(x + _L0_attn_ref(x, L0_attn_Wk, L0_attn_Wv, L0_attn_Wr, L0_attn_Wo, L0_attn_spatial_decay, L0_attn_spatial_first, L0_attn_mix_k, L0_attn_mix_v, L0_attn_mix_r), axis=-1)
    x = _layernorm(x + _L0_ffn_ref(x, L0_ffn_attention_mask, L0_ffn_position_ids, L0_ffn_router_w, L0_ffn_router_b, L0_ffn_wq, L0_ffn_wk, L0_ffn_wv, L0_ffn_wo, L0_ffn_w1, L0_ffn_w2, L0_ffn_ln1, L0_ffn_ln2), axis=-1)
    return x

_drawn_inputs = setup_inputs


def setup_inputs(seed=0):
    import zlib

    import numpy as np

    out = dict(_drawn_inputs(seed))
    spreads = {'L0_ffn_ln1': (1.0, 0.6), 'L0_ffn_ln2': (1.0, 0.6)}
    factors = {'L0_attn_spatial_decay': 8.0,
     'L0_attn_spatial_first': 64.0,
     'L0_attn_mix_k': 2.955,
     'L0_attn_mix_r': 4.559,
     'L0_ffn_router_w': 4.003,
     'L0_ffn_wq': 8.0,
     'L0_ffn_wk': 8.0,
     'L0_ffn_wv': 8.0,
     'L0_ffn_wo': 8.0,
     'L0_ffn_w1': 4.089,
     'L0_ffn_w2': 4.006}
    for name, (base, spread) in spreads.items():
        noise = np.random.default_rng([zlib.crc32(name.encode()), seed]).standard_normal(out[name].shape)
        drawn = base * np.exp(spread * noise) if base else spread * noise
        out[name] = jnp.asarray(drawn.astype(out[name].dtype))
    for name, factor in factors.items():
        out[name] = (out[name] * factor).astype(out[name].dtype)
    return out
```

```python
import concourse.bass as bass
from concourse import mybir
from contextlib import ExitStack

import numpy as np


def rwkv_then_selected_block_kernel(nc, x_tok, x_chan, w_attn, columns, mask_rows, positions,
                                    router_w, router_b, w_qk, w_v, w_o, w_up, w_down,
                                    rho_dram, idx_dram, out):
    fp32 = mybir.dt.float32
    i32 = mybir.dt.int32
    u32 = mybir.dt.uint32
    ALU = mybir.AluOpType
    ACT = mybir.ActivationFunctionType
    AX = mybir.AxisListType

    P = 128
    B, T, C = x_tok.shape
    CC = C // P
    TJ = T // P
    HALF = C // 4
    EPS = 1e-5
    DEN_EXP = 32
    LN2 = 0.6931471805599453

    K = T // 8
    KC = K - 1
    NP = B // 2
    H, HD = 16, 16
    F = w_up.shape[1]
    FC = F // P
    GP = 2
    NG = NP // GP
    MB = mask_rows.shape[0] // 2 // 1024
    TWO_PI_INV = 0.15915494309189535
    C1, C2, C3 = 6.28125, 0.0019340515136718750, 1.2556659146474e-06
    PI = 3.1415925
    HALF_PI = 1.5707963267948966
    MAGIC = 12582912.0
    NEG = -3.0e38

    ctx = ExitStack()
    with ctx:
        def sb(name, shape, dt=fp32):
            return ctx.enter_context(nc.sbuf_tensor(name, shape, dt))

        def sem(name):
            return ctx.enter_context(nc.semaphore(name))

        wa = sb("wa", [P, 4, CC, C])
        wqk = sb("wqk", [P, CC, 2 * C])
        wv = sb("wv", [P, CC, C])
        wo = sb("wo", [P, CC, C])
        wup = sb("wup", [P, CC, F])
        wdn = sb("wdn", [P, FC, C])
        ident = sb("ident", [P, P])
        cols = sb("cols", [P, 4 * CC + 3])
        uw = cols[:, 0:2 * CC].rearrange("p (a c) -> p a c", c=CC)
        gains = cols[:, 2 * CC:4 * CC].rearrange("p (a c) -> p a c", c=CC)
        mix = cols[:, 4 * CC:4 * CC + 3]
        euw = sb("euw", [P, 2, CC])
        ewb = sb("ewb", [P, CC, T])
        rwb = sb("rwb", [P, C])
        rwst = sb("rwst", [P, 8])
        rbb = sb("rbb", [P, 1])
        mhalf = sb("mhalf", [P, 2 * P])
        phalf = sb("phalf", [P, P])
        tick = sb("tick", [P, 1])
        lnbias = sb("lnbias", [P, 2])
        stats_all = sb("stats_all", [P, B, TJ, 3])
        tokall = sb("tokall", [P, 4, B * TJ])

        ARENA = 34000
        arena = sb("arena", [P, ARENA])
        top = [0]

        def place(*shape):
            n = 1
            for s in shape:
                n *= s
            a = arena[:, top[0]:top[0] + n]
            top[0] += n
            assert top[0] <= ARENA, top[0]
            if len(shape) == 2:
                a = a.rearrange("p (a b) -> p a b", b=shape[1])
            elif len(shape) == 3:
                a = a.rearrange("p (a b c) -> p a b c", b=shape[1], c=shape[2])
            return a

        def both(*shape):
            return [place(*shape), place(*shape)]

        xs = [place(T) for _ in range(4)]
        xc = [place(CC, T) for _ in range(4)]
        xm = both(3, T)
        xt = both(TJ, C)
        ek = both(CC, T)
        er = both(CC, T)
        ekv = place(CC, T)
        ab = both(2 * CC, T)
        aa = [x[:, 0:CC, :] for x in ab]
        bb = [x[:, CC:2 * CC, :] for x in ab]
        ld = both(CC, T)
        gg = both(CC, T)
        junk = place(TJ, C)
        diff = place(T)
        st6 = both(TJ, 6)
        stat = both(TJ, 3)
        t2 = both(TJ)
        s2 = both(TJ)
        nm = both(TJ)

        ps = ctx.enter_context(nc.psum_tensor("ps", [P, 8, 512], fp32))
        psK, psR, psV = ps[:, 0:2, :], ps[:, 2:4, :], ps[:, 4:6, :]
        psY = ps[:, 6:8, :].rearrange("p a (j c) -> p (a j) c", c=C)

        wseq = [sb("wseq0", [B, T]), sb("wseq1", [B, T])]
        topv = sb("topv", [B, K])
        topi = sb("topi", [B, K], u32)
        topf = sb("topf", [B, K])
        slots4 = sb("slots4", [B, 4, K])
        bcol = sb("bcol", [P, 4])
        bcol_i = sb("bcol_i", [P, 1], i32)
        sel = sb("sel", [P, 4, NP])
        row_i = sb("row_i", [P, NP], i32)
        pos_i = sb("pos_i", [P, NP], i32)
        msk_i = sb("msk_i", [P, NP], i32)
        rhog = sb("rhog", [P, NP])
        posg = sb("posg", [P, NP], i32)
        posf = sb("posf", [P, NP])
        inv = sb("inv", [P, HD // 2])
        ang = sb("ang", [P, NP * HD // 2])
        trn = sb("trn", [P, 2, NP * HD // 2])
        trg = sb("trg", [P, 2, NP, HD // 2])
        blk = sb("blk", [P, P // HD])
        bm = sb("bm", [P, 2])
        tcol = sb("tcol", [P, TJ])
        ssq = sb("ssq", [P, NP])
        rstd = sb("rstd", [P, NP])
        rstd2 = sb("rstd2", [P, NP])
        fst = sb("fst", [P, 2, GP, 10])
        dtick = sb("dtick", [P, 1])

        top[0] = 0
        xsel = place(NP, C)
        x1 = place(NP, C)
        mall = place(NP, K)
        ib = place(NP, 2 * K)
        after_ib = top[0]
        mrow = [place(T) for _ in range(4)]
        mrt = both(TJ, P)
        oh = both(TJ, P)
        sq = place(NP, C)
        top[0] = after_ib
        hn = both(C)
        hnT = both(CC, P)
        rq = both(2 * C)
        rtmp = place(2 * C)
        qT = both(CC, P)
        kblk = [place(CC, 2 * P) for _ in range(2)]
        vblk = [place(2, H // 2 * 34) for _ in range(2)]
        sc = place(H, K)
        mx = both(H)
        pr = both(H, K)
        pT = both(TJ, 2 * P)
        rd = both(H)
        osb = both(C)
        oT = both(CC, P)
        after_attention = top[0]
        top[0] = after_ib
        h2T = place(CC, NP * P)
        uT = both(FC, GP * P)
        hn2 = both(C)
        x2 = both(GP, C)
        outr = place(NP, C)
        sq2 = outr
        xshare = place(NP, C)

        chan_in = [sem(f"chan_in{p}") for p in range(4)]
        tok_in = [sem(f"tok_in{p}") for p in range(2)]
        row_out = [sem(f"row_out{p}") for p in range(2)]
        w_in = sem("w_in")
        w2_in = sem("w2_in")
        small_in = sem("small_in")
        edges_zero = sem("edges_zero")
        ident_made = sem("ident_made")
        consts_made = sem("consts_made")
        eu_made = sem("eu_made")
        ewb_made = sem("ewb_made")
        rw_chain = sem("rw_chain")
        diff_made = sem("diff_made")
        scaled = sem("scaled")
        mixed = sem("mixed")
        k_ready = sem("k_ready")
        v_ready = sem("v_ready")
        r_ready = sem("r_ready")
        y_ready = sem("y_ready")
        ek_done = sem("ek_done")
        er_done = sem("er_done")
        clamp_done = sem("clamp_done")
        ls_done = sem("ls_done")
        ld_done = sem("ld_done")
        sum_done = sem("sum_done")
        rec_done = sem("rec_done")
        ekv_done = sem("ekv_done")
        scan_done = sem("scan_done")
        den_done = sem("den_done")
        num_done = sem("num_done")
        g_ready = sem("g_ready")
        y_added = sem("y_added")
        bn_done = sem("bn_done")
        aggr_done = sem("aggr_done")
        t2_done = sem("t2_done")
        s2_done = sem("s2_done")
        nm_done = sem("nm_done")
        norm_done = sem("norm_done")
        rows_done = sem("rows_done")
        rope_part = sem("rope_part")
        dve_chain = sem("dve_chain")
        stats_kept = sem("stats_kept")
        s1_in = sem("s1_in")
        s1_out = sem("s1_out")
        root_out = sem("root_out")
        rho_ready = sem("rho_ready")
        w_ready = sem("w_ready")
        w_turned = sem("w_turned")
        wt_copied = sem("wt_copied")
        top_done = sem("top_done")
        idx_stored = sem("idx_stored")
        ib_in = sem("ib_in")
        slots_ready = sem("slots_ready")
        slots_turned = sem("slots_turned")
        idx_ready = sem("idx_ready")
        rho_stored = sem("rho_stored")
        b_iota = sem("b_iota")
        b_made = sem("b_made")
        blk_made = sem("blk_made")
        bm_made = sem("bm_made")
        inv_made = sem("inv_made")
        gathered_rho = sem("gathered_rho")
        gathered_pos = sem("gathered_pos")
        ang_ready = sem("ang_ready")
        sin_done = sem("sin_done")
        rows_in = sem("rows_in")
        x_made = sem("x_made")
        ssq_done = sem("ssq_done")
        rstd_done = sem("rstd_done")
        oh_made = sem("oh_made")
        mt_turned = sem("mt_turned")
        mt_copied = sem("mt_copied")
        mm_done = sem("mm_done")
        mall_done = sem("mall_done")
        mask_loop = sem("mask_loop")
        zero_made = sem("zero_made")
        hn_made = sem("hn_made")
        hn_turned = sem("hn_turned")
        hnT_done = sem("hnT_done")
        qk_ready = sem("qk_ready")
        v_ready2 = sem("v_ready2")
        rope_done = sem("rope_done")
        vblk_done = sem("vblk_done")
        qk_turned = sem("qk_turned")
        qT_done = sem("qT_done")
        kblk_done = sem("kblk_done")
        scores_ready = sem("scores_ready")
        s_done = sem("s_done")
        mx_done = sem("mx_done")
        sub_done = sem("sub_done")
        exp_done = sem("exp_done")
        p_turned = sem("p_turned")
        pT_done = sem("pT_done")
        pv_ready = sem("pv_ready")
        rd_done = sem("rd_done")
        o_done = sem("o_done")
        o_turned = sem("o_turned")
        oT_done = sem("oT_done")
        wo_ready = sem("wo_ready")
        x1_done = sem("x1_done")
        sq2_done = sem("sq2_done")
        ssq2_done = sem("ssq2_done")
        rstd2_done = sem("rstd2_done")
        hn2_made = sem("hn2_made")
        hn2_turned = sem("hn2_turned")
        h2T_done = sem("h2T_done")
        up_ready = sem("up_ready")
        gelu_done = sem("gelu_done")
        dn_ready = sem("dn_ready")
        x2_done = sem("x2_done")
        x2_read = sem("x2_read")
        x2_weighted = sem("x2_weighted")
        fbn_done = sem("fbn_done")
        fag_done = sem("fag_done")
        fvar_done = sem("fvar_done")
        fpow_done = sem("fpow_done")
        fshift_done = sem("fshift_done")
        outr_done = sem("outr_done")
        scattered = sem("scattered")
        mrow_in = [sem(f"mrow_in{k}") for k in range(4)]

        chan_v = x_chan.rearrange("b (c p) t -> b p c t", p=P)
        tok_v = x_tok.rearrange("b (p j) c -> b p j c", j=TJ)
        out_v = out.rearrange("b (p j) c -> b p j c", j=TJ)

        out_rows = out.rearrange("b t c -> (b t) c")

        def rstd_of(tile, at):
            return tile[:, at.n:at.n + 1] if isinstance(at.n, int) else tile[:, bass.ts(at.n, 1)]

        def pair_at(g, i):
            return slice(GP * g.n + i, GP * g.n + i + 1) if isinstance(g.n, int) else bass.ds(g.n * GP + i, 1)

        def first_part_over(eng):
            for par in range(2):
                eng.wait_ge(row_out[par], 16 * (B // 2))

        block = ctx.enter_context(nc.Block())

        RING = 4
        DEPTH = 3

        def periods(eng, period):
            for k in range(RING):
                period(At(0, k))
            with eng.Fori(1, B // RING) as i:
                for k in range(RING):
                    period(At(i, k))
            for k in range(DEPTH):
                period(At(B // RING, k))

        class At:

            def __init__(self, i, k, ring=RING):
                self.i, self.k, self.ring = i + k // ring, k % ring, ring
                self.n = self.i * ring + self.k
                self.par, self.turn = self.k % 2, self.i * (ring // 2) + self.k // 2

            def back(self, d):
                return At(self.i, self.k - d, self.ring)

            def exists(self):
                return not isinstance(self.n, int) or 0 <= self.n < B

            def below(self, count):
                return not isinstance(self.n, int) or self.n < count

            def had(self, d):
                return not isinstance(self.n, int) or self.n >= d

        def pairs(eng, period):
            for k in range(RING):
                period(At(0, k))
            with eng.Fori(1, NP // RING) as i:
                for k in range(RING):
                    period(At(i, k))
            period(At(NP // RING, 0))

        def by_twos(eng, count, step):
            for k in range(2):
                step(At(0, k, 2))
            with eng.Fori(1, count // 2 - 1) as i:
                for k in range(2):
                    step(At(i, k, 2))
            for k in range(2):
                step(At(count // 2 - 1, k, 2))

        def plain(eng, step):
            for k in range(RING):
                step(At(0, k))
            with eng.Fori(1, NP // RING) as i:
                for k in range(RING):
                    step(At(i, k))

        @block.sync
        def _(sp):
            sp.dma_start(cols[:, :], columns).then_inc(small_in, 16)
            sp.dma_start(rwb[:, :], router_w.rearrange("(a c) -> a c", a=1).to_broadcast([P, C])).then_inc(small_in, 16)
            sp.dma_start(rbb[:, :], router_b.rearrange("(a c) -> a c", a=1).to_broadcast([P, 1])).then_inc(small_in, 16)

            def load_channels(s):
                if s.had(RING):
                    sp.wait_ge(r_ready, s.n - (RING - 1))
                else:
                    sp.wait_ge(edges_zero, 2 * RING)
                sp.dma_start(xs[s.k][0:HALF, 1:T], x_chan[s.n, 0:HALF, 0:T - 1]).then_inc(chan_in[s.k], 16)
                sp.dma_start(xs[s.k][HALF:P, 0:T - 1], x_chan[s.n, HALF:P, 1:T]).then_inc(chan_in[s.k], 16)
                sp.dma_start(xc[s.k][:, :, :], chan_v[s.n]).then_inc(chan_in[s.k], 16)

            def load_tokens(s):
                if s.had(2):
                    sp.wait_ge(row_out[s.par], 16 * s.turn)
                sp.dma_start(xt[s.par][:, :, :], tok_v[s.n]).then_inc(tok_in[s.par], 16)

            def period(at):
                if at.back(-2).exists():
                    load_channels(at.back(-2))
                if at.had(1):
                    load_tokens(at.back(1))

            load_channels(At(0, 0))
            sp.dma_start(wa[:, :, :, :], w_attn.rearrange("m (c p) o -> p m c o", p=P)).then_inc(w_in, 16)
            load_channels(At(0, 1))
            for k in range(RING):
                period(At(0, k))
            for dst, src in ((wqk, w_qk), (wv, w_v), (wo, w_o), (wup, w_up), (wdn, w_down)):
                sp.dma_start(dst[:, :, :], src.rearrange("(c p) o -> p c o", p=P)).then_inc(w2_in, 16)
            with sp.Fori(1, B // RING - 1) as i:
                for k in range(RING):
                    period(At(i, k))
            for k in range(RING + 1):
                period(At(B // RING - 1, k))

            sp.wait_ge(rho_ready, 1)
            with nc.allow_non_contiguous_dma(reason="four tokens of a partition at a time"):
                sp.dma_start(rho_dram.rearrange("(b p j) a -> p b (j a)", p=P, j=TJ),
                             tokall[:, 2, :].rearrange("p (b j) -> p b j", j=TJ)).then_inc(rho_stored, 16)
            sp.wait_ge(top_done, 1)
            sp.dma_start(idx_dram, topf[:, :]).then_inc(idx_stored, 16)
            sp.wait_ge(idx_stored, 16)
            first_part_over(sp)
            sp.dma_start(ib.rearrange("p n k -> p (n k)"),
                         idx_dram.rearrange("b k -> (b k)").rearrange("(a n) -> a n", a=1).to_broadcast([P, B * K])).then_inc(ib_in, 16)
            sp.wait_ge(rho_stored, 16)

        @block.gpsimd
        def _(pool):
            g = nc.gpsimd
            g.memset(ident[:, :], 0.0).then_inc(ident_made, 1)
            pool.wait_ge(ident_made, 1)
            g.affine_select(out=ident[:, :], in_=ident[:, :], compare_op=ALU.not_equal, fill=1.0,
                            base=0, pattern=[[-1, P]], channel_multiplier=1).then_inc(ident_made, 1)
            g.memset(mhalf[:, :], -0.5).then_inc(consts_made, 1)
            g.memset(phalf[:, :], 0.5).then_inc(consts_made, 1)
            g.memset(lnbias[:, 0:1], -DEN_EXP * LN2).then_inc(consts_made, 1)
            g.memset(lnbias[:, 1:2], 1e-6).then_inc(consts_made, 1)
            g.iota(bcol_i[:, :], pattern=[[0, 1]], base=0, channel_multiplier=1).then_inc(b_iota, 1)
            for d in range(HD // 2):
                g.memset(inv[:, d:d + 1], float(1.0 / np.float32(10000.0) ** np.float32(2.0 * d / HD))).then_inc(inv_made, 1)
            g.memset(blk[:, :], 0.25).then_inc(blk_made, 1)
            pool.wait_ge(blk_made, 1)
            g.affine_select(out=blk[:, :], in_=blk[:, :], compare_op=ALU.is_ge, fill=0.0, base=0,
                            pattern=[[-HD, P // HD]], channel_multiplier=1).then_inc(blk_made, 1)
            pool.wait_ge(blk_made, 2)
            g.affine_select(out=blk[:, :], in_=blk[:, :], compare_op=ALU.is_ge, fill=0.0, base=HD - 1,
                            pattern=[[HD, P // HD]], channel_multiplier=-1).then_inc(blk_made, 1)
            pool.wait_ge(consts_made, 4)
            pool.wait_ge(small_in, 3 * 16)

            def wait_apart(semaphore, value):
                pool.wait_ge(semaphore, value)
                if not isinstance(value, int):
                    g.tensor_tensor(tick[:, :], mhalf[:, 0:1], phalf[:, 0:1], ALU.add)

            def differences_of(s):
                pool.wait_ge(chan_in[s.k], 48 * (s.i + 1))
                if s.had(2):
                    pool.wait_ge(r_ready, s.n - 1)
                g.tensor_tensor(diff[:, :], xc[s.k][:, 0, :], xs[s.k][:, :], ALU.subtract).then_inc(diff_made, 1)
                wait_apart(diff_made, s.n + 1)
                for m in range(3):
                    last = g.tensor_scalar(xm[s.par][:, m, :], diff[:, :], mix[:, m:m + 1], 0.0, ALU.mult, ALU.add)
                last.then_inc(scaled, 1)

            def mixes_of(s):
                pool.wait_ge(scaled, s.n + 1)
                for m in range(3):
                    last = g.tensor_tensor(xm[s.par][:, m, :], xm[s.par][:, m, :], xs[s.k][:, :], ALU.add)
                last.then_inc(mixed, 1)

            def log_sum_of(s):
                pool.wait_ge(ls_done, s.n + 1)
                g.tensor_tensor(ld[s.par][:, :, :], ld[s.par][:, :, :], er[s.par][:, :, :], ALU.add).then_inc(sum_done, 1)

            def scale_of(s):
                pool.wait_ge(t2_done, s.n + 1)
                if s.had(2):
                    pool.wait_ge(rows_done, s.n - 1)
                g.tensor_tensor(s2[s.par][:, :], t2[s.par][:, :], mhalf[:, 0:TJ], ALU.pow).then_inc(s2_done, 1)

            differences_of(At(0, 0))
            mixes_of(At(0, 0))

            def period(at):
                nxt = at.back(-1)
                if nxt.exists():
                    differences_of(nxt)
                if nxt.exists():
                    mixes_of(nxt)
                if at.had(3) and at.back(3).exists():
                    scale_of(at.back(3))
                if at.had(1) and at.back(1).exists():
                    log_sum_of(at.back(1))

            for k in range(RING):
                period(At(0, k))
            with pool.Fori(1, B // RING - 1) as i:
                for k in range(RING):
                    period(At(i, k))
            for k in range(RING + DEPTH):
                period(At(B // RING - 1, k))

            def store_group(n):
                pool.wait_ge(outr_done, n + 1)
                for q in range(GP * n, GP * (n + 1)):
                    g.indirect_dma_start(out_rows, bass.IndirectOffsetOnAxis(ap=row_i[:, q:q + 1], axis=0),
                                         outr[:, q, :], None).then_inc(scattered, 16)

            pool.wait_ge(s1_in, 2)
            g.tensor_tensor(tokall[:, 0, :], tokall[:, 0, :], mhalf[:, 0:P], ALU.pow).then_inc(s1_out, 1)
            g.tensor_tensor(tokall[:, 1, :], tokall[:, 1, :], phalf[:, :], ALU.pow).then_inc(root_out, 1)
            pool.wait_ge(idx_ready, 3)
            pool.wait_ge(rho_stored, 16)
            first_part_over(pool)
            for q in range(NP):
                g.indirect_dma_start(xsel[:, q, :], None, out_rows,
                                     bass.IndirectOffsetOnAxis(ap=row_i[:, q:q + 1], axis=0)).then_inc(rows_in, 16)
                g.indirect_dma_start(rhog[:, q:q + 1], None, rho_dram,
                                     bass.IndirectOffsetOnAxis(ap=row_i[:, q:q + 1], axis=0)).then_inc(gathered_rho, 16)
                g.indirect_dma_start(posg[:, q:q + 1], None, positions,
                                     bass.IndirectOffsetOnAxis(ap=pos_i[:, q:q + 1], axis=0)).then_inc(gathered_pos, 16)
            for q in range(NP):
                if q >= 4:
                    pool.wait_ge(mt_turned, q - 3)
                g.indirect_dma_start(mrow[q % 4], None, mask_rows,
                                     bass.IndirectOffsetOnAxis(ap=msk_i[:, q:q + 1], axis=0)).then_inc(mrow_in[q % 4], 16)
            for g_ in range(NG):
                pool.wait_ge(fvar_done, g_ + 1)
                g.tensor_tensor(fst[:, g_ % 2, :, 9], fst[:, g_ % 2, :, 8], mhalf[:, 0:GP], ALU.pow).then_inc(fpow_done, 1)
                if g_ >= 1:
                    store_group(g_ - 1)
            store_group(NG - 1)
            pool.wait_ge(scattered, 16 * NP)

        @block.tensor
        def _(pe):
            mm = nc.tensor.matmul

            def projections(s):
                pe.wait_ge(mixed, s.n + 1)
                for m, ps, ready, used in ((0, psK, k_ready, ek_done), (1, psV, v_ready, ekv_done), (2, psR, r_ready, er_done)):
                    if s.had(1):
                        pe.wait_ge(used, s.n)
                    for o in range(CC):
                        for c in range(CC):
                            rhs = xm[s.par][:, m, :] if c == 0 else xc[s.k][:, c, :]
                            last = mm(ps[:, o, :], wa[:, m, c, o * P:(o + 1) * P], rhs, start=(c == 0), stop=(c == CC - 1))
                    last.then_inc(ready, 1)

            def outputs(s):
                pe.wait_ge(g_ready, s.n + 1)
                if s.had(1):
                    pe.wait_ge(y_added, s.n)
                for j in range(TJ):
                    for c in range(CC):
                        last = mm(psY[:, j, :], gg[s.par][:, c, j * P:(j + 1) * P], wa[:, 3, c, :], start=(c == 0), stop=(c == CC - 1))
                last.then_inc(y_ready, 1)

            def period(at):
                if at.exists():
                    projections(at)
                if at.had(2) and at.back(2).exists():
                    outputs(at.back(2))

            pe.wait_ge(w_in, 16)
            periods(pe, period)

            pe.wait_ge(w_ready, 1)
            pe.wait_ge(ident_made, 2)
            pe.wait_ge(y_added, B)
            for j in range(TJ):
                last = nc.tensor.transpose(ps[0:B, 7, j * P:(j + 1) * P], tokall[:, 3, j * B:(j + 1) * B], ident[:, :])
            last.then_inc(w_turned, 1)
            pe.wait_ge(slots_ready, 1)
            for h in range(2):
                for i in range(4):
                    last = mm(ps[h * K:(h + 1) * K, 6, i * NP:(i + 1) * NP], slots4[:, i, :], ident[0:B, h:B:2], start=True, stop=True)
            last.then_inc(slots_turned, 1)
            first_part_over(pe)

            def mask_turn(at):
                pe.wait_ge(mrow_in[at.k], 16 * (at.i + 1))
                if at.had(2):
                    pe.wait_ge(mt_copied, at.n - 1)
                for c in range(TJ):
                    last = nc.tensor.transpose(ps[:, at.par, c * P:(c + 1) * P], mrow[at.k][:, c * P:(c + 1) * P], ident[:, :])
                last.then_inc(mt_turned, 1)

            def mask_pick(at):
                pe.wait_ge(mt_copied, at.n + 1)
                pe.wait_ge(oh_made, at.n + 1)
                if at.had(2):
                    pe.wait_ge(mall_done, at.n - 1)
                for b in range(2):
                    for c in range(TJ):
                        last = mm(ps[b * K:(b + 1) * K, 2 + at.par, 0:K], mrt[at.par][:, c, b * K:(b + 1) * K],
                                  oh[at.par][:, c, b * K:(b + 1) * K], start=(c == 0), stop=(c == TJ - 1))
                last.then_inc(mm_done, 1)

            mask_turn(At(0, 0))

            def mask_period(at):
                if at.back(-1).below(NP):
                    mask_turn(at.back(-1))
                mask_pick(at)

            for k in range(RING):
                mask_period(At(0, k))
            with pe.Fori(1, NP // RING - 1) as i:
                for k in range(RING):
                    mask_period(At(i, k))
            for k in range(RING):
                mask_period(At(NP // RING - 1, k))

            def hn_turn(at):
                pe.wait_ge(hn_made, at.n + 1)
                if at.had(1):
                    pe.wait_ge(hnT_done, at.n)
                for c in range(CC):
                    last = nc.tensor.transpose(ps[:, 6, c * P:(c + 1) * P], hn[at.par][:, c * P:(c + 1) * P], ident[:, :])
                last.then_inc(hn_turned, 1)

            def scores(at):
                pe.wait_ge(qT_done, at.n + 1)
                pe.wait_ge(kblk_done, at.n + 1)
                if at.had(1):
                    pe.wait_ge(s_done, at.n)
                for b in range(2):
                    for c in range(CC):
                        for t in range(4):
                            rows = slice(32 * t, 32 * t + 32)
                            keys = kblk[at.par][rows, c, :].rearrange("p (h k) -> p h k", h=2)
                            last = mm(ps[b * K:(b + 1) * K, t, c * P:(c + 1) * P].rearrange("p (h k) -> p h k", h=2),
                                      qT[at.par][rows, c, b * K:(b + 1) * K], keys[:, :, b * K:(b + 1) * K], start=True, stop=True)
                last.then_inc(scores_ready, 1)

            def projections2(at):
                pe.wait_ge(hnT_done, at.n + 1)
                if at.had(2):
                    pe.wait_ge(x1_done, at.n - 1)
                for c in range(CC):
                    last = mm(ps[:, 7, :], hnT[at.par][:, c, :], wqk[:, c, :], start=(c == 0), stop=(c == CC - 1))
                last.then_inc(qk_ready, 1)
                if at.had(2):
                    pe.wait_ge(o_done, at.n - 1)
                for c in range(CC):
                    last = mm(ps[:, 4, 0:C], hnT[at.par][:, c, :], wv[:, c, :], start=(c == 0), stop=(c == CC - 1))
                last.then_inc(v_ready2, 1)

            def p_turn(at):
                pe.wait_ge(exp_done, at.n + 1)
                if at.had(1):
                    pe.wait_ge(pT_done, at.n)
                for t in range(4):
                    for c in range(CC):
                        last = nc.tensor.transpose(ps[:, t, 256 + c * P:256 + (c + 1) * P],
                                                   pr[at.par].rearrange("p h k -> p (h k)")[:, (t * CC + c) * P:(t * CC + c + 1) * P], ident[:, :])
                last.then_inc(p_turned, 1)

            def qk_turn(at):
                pe.wait_ge(rope_done, at.n + 1)
                if at.had(1):
                    pe.wait_ge(qT_done, at.n)
                    pe.wait_ge(kblk_done, at.n)
                for c in range(4):
                    last = nc.tensor.transpose(ps[:, 5, c * P:(c + 1) * P], rq[at.par][:, c * P:(c + 1) * P], ident[:, :])
                last.then_inc(qk_turned, 1)

            def values(at, before):
                pe.wait_ge(pT_done, at.n + 1)
                pe.wait_ge(vblk_done, before)
                for b in range(2):
                    for hp in range(H // 2):
                        t, c = hp % 4, hp // 4
                        last = mm(ps[b * K:(b + 1) * K, 4, hp * 34:(hp + 1) * 34], pT[at.par][:, t, c * P + b * K:c * P + (b + 1) * K],
                                  vblk[at.par][:, b, hp * 34:(hp + 1) * 34], start=True, stop=True)
                last.then_inc(pv_ready, 1)

            def o_turn(at):
                pe.wait_ge(o_done, at.n + 1)
                if at.had(1):
                    pe.wait_ge(oT_done, at.n)
                for c in range(CC):
                    last = nc.tensor.transpose(ps[:, 6, 256 + c * P:256 + (c + 1) * P], osb[at.par][:, c * P:(c + 1) * P], ident[:, :])
                last.then_inc(o_turned, 1)

            def o_project(at):
                pe.wait_ge(oT_done, at.n + 1)
                for c in range(CC):
                    last = mm(ps[:, 7, 0:C], oT[at.par][:, c, :], wo[:, c, :], start=(c == 0), stop=(c == CC - 1))
                last.then_inc(wo_ready, 1)

            def att_period(at):
                new, old = at.below(NP), at.had(1)
                if new:
                    hn_turn(at)
                if old:
                    scores(at.back(1))
                if new:
                    projections2(at)
                if old:
                    p_turn(at.back(1))
                if new:
                    qk_turn(at)
                if old:
                    values(at.back(1), at.n + 1 if new else at.n)
                    o_turn(at.back(1))
                    o_project(at.back(1))

            pe.wait_ge(w2_in, 5 * 16)
            pairs(pe, att_period)

            def hn2_turn(at):
                pe.wait_ge(hn2_made, at.n + 1)
                if at.had(2):
                    pe.wait_ge(h2T_done, at.n - 1)
                for c in range(CC):
                    last = nc.tensor.transpose(ps[:, 6 + at.par, c * P:(c + 1) * P], hn2[at.par][:, c * P:(c + 1) * P], ident[:, :])
                last.then_inc(hn2_turned, 1)

            plain(pe, hn2_turn)

            def up(g):
                pe.wait_ge(h2T_done, GP * (g.n + 1))
                for k in range(FC // 2):
                    if g.had(1):
                        pe.wait_ge(gelu_done, FC // 2 * (g.n - 1) + k + 1)
                    for h in range(2):
                        f = 2 * k + h
                        for c in range(CC):
                            last = mm(ps[:, k, h * GP * P:(h + 1) * GP * P], wup[:, c, f * P:(f + 1) * P],
                                      h2T[:, c, bass.ts(g.n, GP * P)], start=(c == 0), stop=(c == CC - 1))
                    last.then_inc(up_ready, 1)

            def down(g):
                pe.wait_ge(gelu_done, FC // 2 * (g.n + 1))
                if g.had(2):
                    pe.wait_ge(x2_read, g.n - 1)
                for i in range(GP):
                    for f in range(FC):
                        last = mm(ps[:, 4 + g.par, i * C:(i + 1) * C], uT[g.par][:, f, i * P:(i + 1) * P], wdn[:, f, :],
                                  start=(f == 0), stop=(f == FC - 1))
                last.then_inc(dn_ready, 1)

            def mlp_period(g):
                if g.back(-1).below(NG):
                    up(g.back(-1))
                down(g)

            up(At(0, 0, 2))
            by_twos(pe, NG, mlp_period)

        @block.scalar
        def _(act):
            a = nc.scalar
            a.preload_act_table_set("natural_log_exp_and_others")
            act.wait_ge(small_in, 3 * 16)
            a.activation(euw[:, :, :], uw, ACT.Exp, scale=1.0 / T).then_inc(eu_made, 1)
            act.wait_ge(consts_made, 4)

            def exp_k_of(s):
                act.wait_ge(k_ready, s.n + 1)
                if s.had(2):
                    act.wait_ge(den_done, s.n - 1)
                a.activation(ek[s.par][:, :, :], psK[:, :, :], ACT.Exp).then_inc(ek_done, 1)

            def exp_r_of(s):
                act.wait_ge(r_ready, s.n + 1)
                if s.had(2):
                    act.wait_ge(sum_done, s.n - 1)
                a.activation(er[s.par][:, :, :], psR[:, :, :], ACT.Exp, scale=-1.0).then_inc(er_done, 1)

            def ln_den_of(s):
                act.wait_ge(den_done, s.n + 1)
                if s.had(2):
                    act.wait_ge(g_ready, s.n - 1)
                a.activation(ld[s.par][:, :, :], bb[s.par][:, :, :], ACT.Ln, scale=2.0 ** -DEN_EXP).then_inc(ld_done, 1)

            def ln_gate_of(s):
                act.wait_ge(clamp_done, s.n + 1)
                a.activation(er[s.par][:, :, :], er[s.par][:, :, :], ACT.Ln, bias=1.0).then_inc(ls_done, 1)

            def reciprocal_of(s):
                act.wait_ge(sum_done, s.n + 1)
                a.activation(ld[s.par][:, :, :], ld[s.par][:, :, :], ACT.Exp, scale=-1.0, bias=lnbias[:, 0:1]).then_inc(rec_done, 1)

            def rows_of(s):
                act.wait_ge(nm_done, s.n + 1)
                for j in range(TJ):
                    last = a.activation(xt[s.par][:, j, :], xt[s.par][:, j, :], ACT.Identity,
                                        scale=s2[s.par][:, j:j + 1], bias=nm[s.par][:, j:j + 1])
                last.then_inc(rows_done, 1)
                act.wait_ge(rows_done, s.n + 1)
                act.dma_start(out_v[s.n], xt[s.par][:, :, :]).then_inc(row_out[s.par], 16)

            def period(at):
                if at.exists():
                    exp_k_of(at)
                if at.had(1) and at.back(1).exists():
                    reciprocal_of(at.back(1))
                if at.exists():
                    exp_r_of(at)
                    ln_den_of(at)
                    ln_gate_of(at)
                if at.had(3) and at.back(3).exists():
                    rows_of(at.back(3))

            periods(act, period)

            act.wait_ge(slots_ready, 1)
            first_part_over(act)
            act.wait_ge(ang_ready, 1)
            a.activation(trg[:, :, :, :].rearrange("p a n d -> p (a n d)"), trn[:, :, :].rearrange("p a n -> p (a n)"), ACT.Sin).then_inc(sin_done, 1)
            a.preload_act_table_set("natural_log_exp_and_others")
            act.wait_ge(ssq_done, 1)
            a.activation(rstd[:, :], ssq[:, :], ACT.Ln, scale=1.0 / C, bias=lnbias[:, 1:2]).then_inc(rstd_done, 1)
            act.wait_ge(rstd_done, 1)
            a.activation(rstd[:, :], rstd[:, :], ACT.Exp, scale=-0.5).then_inc(rstd_done, 1)

            def mask_copy(at):
                act.wait_ge(mt_turned, at.n + 1)
                if at.had(2):
                    act.wait_ge(mm_done, at.n - 1)
                a.activation(mrt[at.par].rearrange("p c k -> p (c k)"), ps[:, at.par, :], ACT.Copy).then_inc(mt_copied, 1)

            plain(act, mask_copy)

            def hnT_copy(at):
                act.wait_ge(hn_turned, at.n + 1)
                if at.had(2):
                    act.wait_ge(v_ready2, at.n - 1)
                for c in range(CC):
                    last = a.activation(hnT[at.par][:, c, :], ps[:, 6, c * P:(c + 1) * P], ACT.Copy, scale=gains[:, 0, c:c + 1])
                last.then_inc(hnT_done, 1)

            def v_copy(at):
                act.wait_ge(v_ready2, at.n + 1)
                if at.had(2):
                    act.wait_ge(pv_ready, at.n - 1)
                for b in range(2):
                    for h in range(2):
                        dst = vblk[at.par][h * K:(h + 1) * K, b, :].rearrange("p (n d) -> p n d", d=34)[:, :, h * HD:(h + 1) * HD]
                        src = ps[b * K:(b + 1) * K, 4, 0:C].rearrange("p (n d) -> p n d", d=2 * HD)[:, :, h * HD:(h + 1) * HD]
                        last = a.activation(dst, src, ACT.Copy)
                last.then_inc(vblk_done, 1)

            def exp_p(at):
                act.wait_ge(sub_done, at.n + 1)
                if at.had(2):
                    act.wait_ge(p_turned, at.n - 1)
                a.activation(pr[at.par][:, :, 0:KC], sc[:, :, 0:KC], ACT.Exp).then_inc(exp_done, 1)

            def q_copy(at):
                act.wait_ge(qk_turned, at.n + 1)
                if at.had(2):
                    act.wait_ge(scores_ready, at.n - 1)
                a.activation(qT[at.par].rearrange("p c k -> p (c k)"), ps[:, 5, 0:CC * P], ACT.Copy).then_inc(qT_done, 1)

            def k_copy(at):
                for h in range(2):
                    last = a.activation(kblk[at.par][:, :, h * P:(h + 1) * P], ps[:, 5, CC * P:2 * CC * P].rearrange("p (c k) -> p c k", c=CC),
                                        ACT.Copy, scale=bm[:, h:h + 1])
                last.then_inc(kblk_done, 1)

            def pT_copy(at):
                act.wait_ge(p_turned, at.n + 1)
                if at.had(2):
                    act.wait_ge(pv_ready, at.n - 1)
                a.activation(pT[at.par], ps[:, 0:4, 256:512], ACT.Copy).then_inc(pT_done, 1)

            def oT_copy(at):
                act.wait_ge(o_turned, at.n + 1)
                if at.had(2):
                    act.wait_ge(wo_ready, at.n - 1)
                a.activation(oT[at.par].rearrange("p c k -> p (c k)"), ps[:, 6, 256:512], ACT.Copy).then_inc(oT_done, 1)

            def att_period(at):
                new, old = at.below(NP), at.had(1)
                if new:
                    hnT_copy(at)
                    v_copy(at)
                if old:
                    exp_p(at.back(1))
                if new:
                    q_copy(at)
                    k_copy(at)
                if old:
                    pT_copy(at.back(1))
                    oT_copy(at.back(1))

            act.wait_ge(bm_made, 1)
            act.wait_ge(zero_made, 1)
            pairs(act, att_period)

            act.wait_ge(ssq2_done, 1)
            a.activation(rstd2[:, :], ssq[:, :], ACT.Ln, scale=1.0 / C, bias=lnbias[:, 1:2]).then_inc(rstd2_done, 1)
            act.wait_ge(rstd2_done, 1)
            a.activation(rstd2[:, :], rstd2[:, :], ACT.Exp, scale=-0.5).then_inc(rstd2_done, 1)
            a.preload_act_table(ACT.Gelu_apprx_tanh)

            def h2T_copy(at):
                act.wait_ge(hn2_turned, at.n + 1)
                for c in range(CC):
                    last = a.activation(h2T[:, c, bass.ts(at.n, P)], ps[:, 6 + at.par, c * P:(c + 1) * P], ACT.Copy, scale=gains[:, 1, c:c + 1])
                last.then_inc(h2T_done, 1)

            plain(act, h2T_copy)

            def gelu_of(g):
                if g.had(2):
                    act.wait_ge(dn_ready, g.n - 1)
                for k in range(FC // 2):
                    act.wait_ge(up_ready, FC // 2 * g.n + k + 1)
                    a.activation(uT[g.par][:, 2 * k:2 * k + 2, :].rearrange("p f n -> p (f n)"), ps[:, k, :], ACT.Gelu_apprx_tanh).then_inc(gelu_done, 1)

            by_twos(act, NG, gelu_of)

        @block.vector
        def _(dve):
            v = nc.vector
            for k in range(RING):
                v.memset(xs[k][0:HALF, 0:1], 0.0).then_inc(edges_zero, 1)
                v.memset(xs[k][HALF:P, T - 1:T], 0.0).then_inc(edges_zero, 1)
            v.memset(ewb[:, :, :], 1.0).then_inc(ewb_made, 1)
            dve.wait_ge(ewb_made, 1)
            dve.wait_ge(eu_made, 1)
            dve.wait_ge(blk_made, 3)
            v.reduce_sum(bm[:, :], blk[:, :].rearrange("p (n h) -> p h n", h=2), AX.X).then_inc(bm_made, 1)
            for c in range(CC):
                v.tensor_scalar(ewb[:, c, :], ewb[:, c, :], euw[:, 1, c:c + 1], None, ALU.mult).then_inc(ewb_made, 1)
            v.bn_stats(rwst[:, 0:6], rwb[:, :]).then_inc(rw_chain, 1)
            dve.wait_ge(rw_chain, 1)
            v.bn_aggr(rwst[:, 6:8], rwst[:, 0:6]).then_inc(rw_chain, 1)
            dve.wait_ge(rw_chain, 2)
            v.tensor_scalar(rwb[:, :], rwb[:, :], rwst[:, 6:7], None, ALU.subtract).then_inc(rw_chain, 1)
            dve.wait_ge(rw_chain, 3)
            dve.wait_ge(ewb_made, 1 + CC)

            def recurrence_of(s):
                par = s.par
                dve.wait_ge(v_ready, s.n + 1)
                dve.wait_ge(ek_done, s.n + 1)
                v.tensor_tensor(ekv[:, :, :], ek[par][:, :, :], psV[:, :, :], ALU.mult).then_inc(ekv_done, 1)
                if s.had(2):
                    dve.wait_ge(ld_done, s.n - 1)
                    dve.wait_ge(g_ready, s.n - 1)
                v.memset(ab[par][:, :, 0:1], 0.0)
                for c in range(CC):
                    v.tensor_tensor_scan(bb[par][:, c, 1:T], ewb[:, c, 0:T - 1], ek[par][:, c, 0:T - 1], 0.0, ALU.mult, ALU.add)
                dve.wait_ge(ekv_done, s.n + 1)
                for c in range(CC):
                    last = v.tensor_tensor_scan(aa[par][:, c, 1:T], ewb[:, c, 0:T - 1], ekv[:, c, 0:T - 1], 0.0, ALU.mult, ALU.add)
                last.then_inc(scan_done, 1)
                dve.wait_ge(scan_done, s.n + 1)
                for c in range(CC):
                    last = v.scalar_tensor_tensor(bb[par][:, c, :], ek[par][:, c, :], euw[:, 0, c:c + 1], bb[par][:, c, :], ALU.mult, ALU.add)
                last.then_inc(den_done, 1)
                for c in range(CC):
                    last = v.scalar_tensor_tensor(aa[par][:, c, :], ekv[:, c, :], euw[:, 0, c:c + 1], aa[par][:, c, :], ALU.mult, ALU.add)
                last.then_inc(num_done, 1)

            def clamp_of(s):
                dve.wait_ge(er_done, s.n + 1)
                v.tensor_scalar(er[s.par][:, :, :], er[s.par][:, :, :], 2.0 ** 62, None, ALU.min).then_inc(clamp_done, 1)

            def gate_of(s):
                par = s.par
                dve.wait_ge(rec_done, s.n + 1)
                if s.had(2):
                    dve.wait_ge(y_ready, s.n - 1)
                dve.wait_ge(num_done, s.n + 1)
                for c in range(CC):
                    last = v.tensor_tensor(gg[par][:, c, :].rearrange("p (j q) -> p q j", j=TJ),
                                           aa[par][:, c, :].rearrange("p (q j) -> p q j", j=TJ),
                                           ld[par][:, c, :].rearrange("p (q j) -> p q j", j=TJ), ALU.mult)
                last.then_inc(g_ready, 1)

            def statistics_of(s):
                par = s.par
                dve.wait_ge(y_ready, s.n + 1)
                dve.wait_ge(tok_in[par], 16 * (s.turn + 1))
                v.tensor_tensor(xt[par][:, :, :], psY[:, :, :], xt[par][:, :, :], ALU.add).then_inc(y_added, 1)
                dve.wait_ge(y_added, s.n + 1)
                for j in range(TJ):
                    last = v.bn_stats(st6[par][:, j, :], xt[par][:, j, :])
                last.then_inc(bn_done, 1)
                for j in range(TJ):
                    if j == TJ - 1:
                        dve.wait_ge(bn_done, s.n + 1)
                    v.tensor_tensor_reduce(junk[:, j, :], xt[par][:, j, :], rwb[:, :], 1.0, 0.0, ALU.mult, ALU.add,
                                           stat[par][:, j, 2:3])
                for j in range(TJ):
                    last = v.bn_aggr(stat[par][:, j, 0:2], st6[par][:, j, :])
                last.then_inc(aggr_done, 1)
                dve.wait_ge(aggr_done, s.n + 1)
                v.tensor_scalar(t2[par][:, :], stat[par][:, :, 1], 1.0 + EPS / 4, EPS * EPS / 4, ALU.mult, ALU.add).then_inc(t2_done, 1)
                v.tensor_copy(stats_all[:, s.n, :, :], stat[par][:, :, :]).then_inc(stats_kept, 1)

            def shift_of(s):
                dve.wait_ge(s2_done, s.n + 1)
                v.scalar_tensor_tensor(nm[s.par][:, :], stat[s.par][:, :, 0], -1.0, s2[s.par][:, :], ALU.mult, ALU.mult).then_inc(nm_done, 1)

            def period(at):
                if at.exists():
                    recurrence_of(at)
                if at.exists():
                    clamp_of(at)
                if at.had(1) and at.back(1).exists():
                    gate_of(at.back(1))
                if at.had(3) and at.back(3).exists():
                    shift_of(at.back(3))
                if at.had(2) and at.back(2).exists():
                    statistics_of(at.back(2))

            periods(dve, period)

            n_chain = [0]

            def link(ins):
                n_chain[0] += 1
                ins.then_inc(dve_chain, 1)
                dve.wait_ge(dve_chain, n_chain[0])

            var = stats_all[:, :, :, 1]
            tok = [tokall[:, i, :].rearrange("p (b j) -> p b j", j=TJ) for i in range(4)]
            dve.wait_ge(stats_kept, B)
            v.tensor_scalar(tok[0], var, EPS, None, ALU.add).then_inc(s1_in, 1)
            v.tensor_scalar(tok[1], var, 1.0 + EPS / 4, EPS * EPS / 4, ALU.mult, ALU.add).then_inc(s1_in, 1)
            dve.wait_ge(s1_out, 1)
            by_j = tokall[:, 3, :].rearrange("p (j b) -> p b j", j=TJ)
            link(v.tensor_tensor(by_j, stats_all[:, :, :, 2], tok[0], ALU.mult))
            v.tensor_scalar(tokall[:, 3, :], tokall[:, 3, :], rbb[:, 0:1], None, ALU.add).then_inc(w_ready, 1)
            dve.wait_ge(root_out, 1)
            v.tensor_tensor(tok[2], tok[0], tok[1], ALU.mult).then_inc(rho_ready, 1)
            dve.wait_ge(w_turned, 1)
            link(v.tensor_copy(wseq[0][:, :].rearrange("b (p j) -> b j p", j=TJ), ps[0:B, 7, :].rearrange("b (j p) -> b j p", j=TJ)))
            for r in range(K // 8):
                eight = slice(8 * r, 8 * r + 8)
                link(v.max(topv[:, eight], wseq[r % 2][:, :]))
                link(v.max_index(topi[:, eight], topv[:, eight], wseq[r % 2][:, :]))
                if r < K // 8 - 1:
                    link(v.match_replace(wseq[1 - r % 2][:, :], topv[:, eight], wseq[r % 2][:, :], NEG))
            v.tensor_copy(topf[:, :], topi[:, :]).then_inc(top_done, 1)
            dve.wait_ge(top_done, 1)
            dve.wait_ge(b_iota, 1)
            link(v.tensor_copy(bcol[:, 0:1], bcol_i[:, :]))
            link(v.tensor_scalar(bcol[:, 1:2], bcol[:, 0:1], float(T), None, ALU.mult))
            link(v.tensor_scalar(bcol[:, 2:3], bcol[:, 0:1], float(MB - 1), 1024.0, ALU.min, ALU.mult))
            for c in range(TJ):
                v.tensor_scalar(tcol[:, c:c + 1], bcol[:, 0:1], float(c * P), None, ALU.add)
            link(v.tensor_scalar(slots4[:, 3, :], topv[:, :], topv[:, K - 1:K], -1.0, ALU.is_gt, ALU.mult))
            link(v.tensor_scalar(slots4[:, 3, :], slots4[:, 3, :], 2.0, None, ALU.add))
            link(v.tensor_scalar(slots4[:, 0, :], topf[:, :], bcol[0:B, 1:2], None, ALU.add))
            link(v.tensor_scalar(slots4[:, 1, :], topf[:, :], bcol[0:B, 2:3], None, ALU.add))
            link(v.tensor_copy(slots4[:, 2, 0:KC], topv[:, 0:KC]))
            v.memset(slots4[:, 2, KC:K], 0.0).then_inc(slots_ready, 1)
            dve.wait_ge(slots_turned, 1)
            link(v.tensor_copy(sel[:, :, :].rearrange("p a n -> p (a n)"), ps[:, 6, 0:4 * NP]))
            v.tensor_copy(row_i[:, :], sel[:, 0, :]).then_inc(idx_ready, 1)
            v.tensor_copy(pos_i[:, :], sel[:, 1, :]).then_inc(idx_ready, 1)
            v.tensor_scalar(msk_i[:, :], sel[:, 1, :], 2.0, None, ALU.mult).then_inc(idx_ready, 1)

            dve.wait_ge(gathered_pos, 16 * NP)
            link(v.tensor_copy(posf[:, :], posg[:, :]))
            dve.wait_ge(inv_made, HD // 2)
            HF = HD // 2
            link(v.tensor_tensor(ang[:, :].rearrange("p (n d) -> p n d", d=HF), posf[:, :].unsqueeze(2).to_broadcast([P, NP, HF]),
                                 inv[:, :].unsqueeze(1).to_broadcast([P, NP, HF]), ALU.mult))
            link(v.tensor_scalar(trn[:, 0, :], ang[:, :], TWO_PI_INV, 0.25, ALU.mult, ALU.add))
            link(v.tensor_scalar(trn[:, 1, :], ang[:, :], TWO_PI_INV, None, ALU.mult))
            link(v.tensor_scalar(trn[:, :, :], trn[:, :, :], MAGIC, MAGIC, ALU.add, ALU.subtract))
            trf = trg[:, :, :, :].rearrange("p a n d -> p a (n d)")
            twice = ang[:, :].unsqueeze(1).to_broadcast([P, 2, NP * HF])
            link(v.scalar_tensor_tensor(trf, trn[:, :, :], -C1, twice, ALU.mult, ALU.add))
            link(v.scalar_tensor_tensor(trf, trn[:, :, :], -C2, trf, ALU.mult, ALU.add))
            link(v.scalar_tensor_tensor(trf, trn[:, :, :], -C3, trf, ALU.mult, ALU.add))
            link(v.tensor_scalar(trf[:, 0, :], trf[:, 0, :], HALF_PI, None, ALU.add))
            v.tensor_scalar(trn[:, :, :], trf, PI, -PI, ALU.min, ALU.max).then_inc(ang_ready, 1)

            dve.wait_ge(rows_in, 16 * NP)
            dve.wait_ge(gathered_rho, 16 * NP)
            link(v.tensor_tensor(xsel, xsel, rhog[:, :].unsqueeze(2).to_broadcast([P, NP, C]), ALU.mult))
            link(v.tensor_tensor(sq, xsel, xsel, ALU.mult))
            v.reduce_sum(ssq[:, :], sq, AX.X).then_inc(ssq_done, 1)

            def one_hot(at):
                if at.had(2):
                    dve.wait_ge(mm_done, at.n - 1)
                v.tensor_tensor(oh[at.par], ib[:, at.n, :].unsqueeze(1).to_broadcast([P, TJ, P]),
                                tcol[:, :].unsqueeze(2).to_broadcast([P, TJ, P]), ALU.is_equal).then_inc(oh_made, 1)

            def mask_keep(at):
                dve.wait_ge(mm_done, at.n + 1)
                v.tensor_copy(mall[:, at.n, :], ps[:, 2 + at.par, 0:K]).then_inc(mall_done, 1)

            def mask_period(at):
                if at.back(-1).below(NP):
                    one_hot(at.back(-1))
                mask_keep(at)

            dve.wait_ge(ib_in, 16)
            one_hot(At(0, 0))
            for k in range(RING):
                mask_period(At(0, k))
            with dve.Fori(1, NP // RING - 1) as i:
                for k in range(RING):
                    mask_period(At(i, k))
            for k in range(RING):
                mask_period(At(NP // RING - 1, k))

            dve.wait_ge(rstd_done, 2)
            dve.wait_ge(mall_done, NP)
            dve.wait_ge(sin_done, 1)
            for par in range(2):
                link(v.memset(vblk[par], 0.0))
                for h in range(2):
                    link(v.memset(vblk[par][h * K:(h + 1) * K, :, :].rearrange("p b (n d) -> p (b n) d", d=34)[:, :, 32 + h:33 + h], 1.0))
                link(v.memset(pr[par][:, :, KC:K], 0.0))
            v.memset(rd[0], 0.0).then_inc(zero_made, 1)

            def normed(at):
                if at.had(2):
                    dve.wait_ge(hn_turned, at.n - 1)
                v.tensor_scalar(hn[at.par], xsel[:, at.n, :], rstd_of(rstd, at), None, ALU.mult).then_inc(hn_made, 1)

            def softmax_in(at):
                dve.wait_ge(scores_ready, at.n + 1)
                if at.had(1):
                    dve.wait_ge(exp_done, at.n)
                mask = mall[:, at.n, :].unsqueeze(1).unsqueeze(1).to_broadcast([P, 4, 4, K])
                v.tensor_tensor(sc.rearrange("p (t h) k -> p t h k", t=4), ps[:, 0:4, 0:256].rearrange("p t (h k) -> p t h k", k=K),
                                mask, ALU.add).then_inc(s_done, 1)
                dve.wait_ge(s_done, at.n + 1)
                v.tensor_reduce(mx[at.par], sc[:, :, 0:KC], AX.X, ALU.max).then_inc(mx_done, 1)
                dve.wait_ge(mx_done, at.n + 1)
                v.tensor_tensor(sc[:, :, 0:KC], sc[:, :, 0:KC], mx[at.par].unsqueeze(2).to_broadcast([P, H, KC]),
                                ALU.subtract).then_inc(sub_done, 1)

            def rope(at):
                dve.wait_ge(qk_ready, at.n + 1)
                if at.had(2):
                    dve.wait_ge(qk_turned, at.n - 1)
                src = ps[:, 7, :].rearrange("p (h a d) -> p h a d", a=2, d=HF)
                dst = rq[at.par].rearrange("p (h a d) -> p h a d", a=2, d=HF)
                tmp = rtmp.rearrange("p (h a d) -> p h a d", a=2, d=HF)
                cos = trg[:, 0, at.n, :].unsqueeze(1)
                sin = trg[:, 1, at.n, :].unsqueeze(1)
                v.tensor_tensor(dst, src, cos.unsqueeze(1).to_broadcast([P, 2 * H, 2, HF]), ALU.mult)
                for half in range(2):
                    last = v.tensor_tensor(tmp[:, :, half, :], src[:, :, 1 - half, :], sin.to_broadcast([P, 2 * H, HF]), ALU.mult)
                last.then_inc(rope_part, 1)
                dve.wait_ge(rope_part, at.n + 1)
                for half, op in ((0, ALU.subtract), (1, ALU.add)):
                    last = v.tensor_tensor(dst[:, :, half, :], dst[:, :, half, :], tmp[:, :, half, :], op)
                last.then_inc(rope_done, 1)

            def output_of(at):
                dve.wait_ge(pv_ready, at.n + 1)
                o = ps[:, 4, 0:H // 2 * 34].rearrange("p (n d) -> p n d", d=34)
                v.reciprocal(rd[at.par].rearrange("p (n h) -> p n h", h=2), o[:, :, 32:34]).then_inc(rd_done, 1)
                dve.wait_ge(rd_done, at.n + 1)
                if at.had(2):
                    dve.wait_ge(o_turned, at.n - 1)
                v.tensor_tensor(osb[at.par].rearrange("p (n h d) -> p n h d", h=2, d=HD), o[:, :, 0:32].rearrange("p n (h d) -> p n h d", h=2),
                                rd[at.par].rearrange("p (n h) -> p n h", h=2).unsqueeze(3).to_broadcast([P, H // 2, 2, HD]),
                                ALU.mult).then_inc(o_done, 1)

            def residual(at):
                dve.wait_ge(wo_ready, at.n + 1)
                v.tensor_tensor(x1[:, at.n, :], ps[:, 7, 0:C], xsel[:, at.n, :], ALU.add).then_inc(x1_done, 1)

            def att_period(at):
                new, old = at.below(NP), at.had(1)
                if old:
                    softmax_in(at.back(1))
                if new:
                    rope(at)
                if at.back(-1).below(NP):
                    normed(at.back(-1))
                if old:
                    output_of(at.back(1))
                    residual(at.back(1))

            normed(At(0, 0))
            for k in range(RING):
                att_period(At(0, k))
            with dve.Fori(1, NP // RING - 1) as i:
                for k in range(RING):
                    att_period(At(i, k))
            for k in range(RING + 1):
                att_period(At(NP // RING - 1, k))

            dve.wait_ge(x1_done, NP)
            link(v.tensor_tensor(sq2, x1, x1, ALU.mult))
            v.tensor_tensor(xshare, xsel, sel[:, 3, :].unsqueeze(2).to_broadcast([P, NP, C]), ALU.mult)
            v.reduce_sum(ssq[:, :], sq2, AX.X).then_inc(ssq2_done, 1)
            dve.wait_ge(rstd2_done, 2)

            def normed2(at):
                if at.had(2):
                    dve.wait_ge(hn2_turned, at.n - 1)
                v.tensor_scalar(hn2[at.par], x1[:, at.n, :], rstd_of(rstd2, at), None, ALU.mult).then_inc(hn2_made, 1)

            plain(dve, normed2)

            def finish(g):
                x2g, f, pair0 = x2[g.par], fst[:, g.par, :, :], bass.ts(g.n, GP)
                dve.wait_ge(dn_ready, g.n + 1)
                v.tensor_tensor(x2g, ps[:, 4 + g.par, :].rearrange("p (i c) -> p i c", c=C), x1[:, pair0, :], ALU.add).then_inc(x2_read, 1)
                dve.wait_ge(x2_read, g.n + 1)
                v.tensor_tensor(x2g, x2g, sel[:, 2, pair0].unsqueeze(2).to_broadcast([P, GP, C]), ALU.mult).then_inc(x2_weighted, 1)
                dve.wait_ge(x2_weighted, g.n + 1)
                v.tensor_tensor(x2g, x2g, xshare[:, pair0, :], ALU.add).then_inc(x2_done, 1)
                dve.wait_ge(x2_done, g.n + 1)
                for i in range(GP):
                    last = v.bn_stats(f[:, i, 0:6], x2g[:, i, :])
                last.then_inc(fbn_done, 1)
                dve.wait_ge(fbn_done, g.n + 1)
                v.memset(dtick[:, :], 0.0)
                for i in range(GP):
                    last = v.bn_aggr(f[:, i, 6:8], f[:, i, 0:6])
                last.then_inc(fag_done, 1)
                dve.wait_ge(fag_done, g.n + 1)
                v.tensor_scalar(f[:, :, 8], f[:, :, 7], EPS, None, ALU.add).then_inc(fvar_done, 1)
                dve.wait_ge(fpow_done, g.n + 1)
                for i in range(GP):
                    last = v.tensor_scalar(outr[:, pair_at(g, i), :].rearrange("p a c -> p (a c)"), x2g[:, i, :],
                                           f[:, i, 6:7], f[:, i, 9:10], ALU.subtract, ALU.mult)
                last.then_inc(outr_done, 1)

            by_twos(dve, NG, finish)


def kernel(**inputs):
    import numpy as np
    import concourse.bacc as bacc
    from concourse import mybir as mb
    from concourse.bass_utils import run_bass_kernel_spmd as run

    nc = bacc.Bacc("TRN2", target_bir_lowering=False, num_devices=1)
    x = np.asarray(inputs["L0_attn_x"])
    arrays = {
        "x_tok": x,
        "x_chan": x.transpose(0, 2, 1),
        "w_attn": np.stack([np.asarray(inputs["L0_attn_" + n]).T for n in ("Wk", "Wv", "Wr", "Wo")]),
        "columns": np.concatenate(
            [np.asarray(inputs["L0_" + n]).reshape(-1, 128).T for n in ("attn_spatial_first", "attn_spatial_decay", "ffn_ln1", "ffn_ln2")]
            + [np.asarray(inputs["L0_attn_mix_" + n])[:128, None] for n in "kvr"], axis=1),
        "mask_rows": np.asarray(inputs["L0_ffn_attention_mask"]).reshape(-1, 512),
        "positions": np.asarray(inputs["L0_ffn_position_ids"]).reshape(-1, 1),
        "router_w": np.asarray(inputs["L0_ffn_router_w"]).reshape(-1),
        "router_b": inputs["L0_ffn_router_b"],
        "w_qk": np.concatenate([inputs["L0_ffn_wq"], inputs["L0_ffn_wk"]], axis=1),
        "w_v": inputs["L0_ffn_wv"],
        "w_o": inputs["L0_ffn_wo"],
        "w_up": inputs["L0_ffn_w1"],
        "w_down": inputs["L0_ffn_w2"],
    }
    arrays = {n: np.ascontiguousarray(a) for n, a in arrays.items()}
    aps = [nc.dram_tensor(n, a.shape, mb.dt.from_np(a.dtype), kind="ExternalInput").ap() for n, a in arrays.items()]
    rho = nc.dram_tensor("rho_scratch", (x.shape[0] * x.shape[1], 1), mb.dt.float32).ap()
    idx = nc.dram_tensor("idx_scratch", (32, 64), mb.dt.float32).ap()
    out = nc.dram_tensor("out", x.shape, mb.dt.float32, kind="ExternalOutput").ap()
    rwkv_then_selected_block_kernel(nc, *aps, rho, idx, out)
    return run(nc, [arrays], core_ids=[0]).results[0]["out"]
```

```python
import concourse.bass as bass
from concourse import mybir
from contextlib import ExitStack

import numpy as np


def rwkv_then_selected_block_kernel(nc, x_tok, x_chan, w_attn, columns, mask_rows, positions,
                                    router_w, router_b, w_qk, w_v, w_o, w_up, w_down,
                                    out):
    fp32 = mybir.dt.float32
    i32 = mybir.dt.int32
    u32 = mybir.dt.uint32
    ALU = mybir.AluOpType
    ACT = mybir.ActivationFunctionType
    AX = mybir.AxisListType

    P = 128
    B, T, C = x_tok.shape
    CC = C // P
    TJ = T // P
    HALF = C // 4
    EPS = 1e-5
    RING = 4
    DEN_EXP = 32
    LN2 = 0.6931471805599453

    K = T // 8
    KC = K - 1
    NP = B // 2
    H, HD = 16, 16
    F = w_up.shape[1]
    FC = F // P
    GP = 2
    NG = NP // GP
    S = 1024
    MB = positions.shape[0] // S
    TWO_PI_INV = 0.15915494309189535
    C1, C2, C3 = 6.28125, 0.0019340515136718750, 1.2556659146474e-06
    PI = 3.1415925
    HALF_PI = 1.5707963267948966
    MAGIC = 12582912.0
    NEG = -3.0e38

    ctx = ExitStack()
    with ctx:
        def sb(name, shape, dt=fp32):
            return ctx.enter_context(nc.sbuf_tensor(name, shape, dt))

        def sem(name):
            return ctx.enter_context(nc.semaphore(name))

        wa = sb("wa", [P, 4, CC, C])
        wqk = sb("wqk", [P, CC, 2 * C])
        wv = sb("wv", [P, CC, C])
        wo = sb("wo", [P, CC, C])
        ident = sb("ident", [P, P])
        cols = sb("cols", [P, 4 * CC + 3])
        uw = cols[:, 0:2 * CC].rearrange("p (a c) -> p a c", c=CC)
        gains = cols[:, 2 * CC:4 * CC].rearrange("p (a c) -> p a c", c=CC)
        mix = cols[:, 4 * CC:4 * CC + 3]
        euw = sb("euw", [P, 2, CC])
        ewb = sb("ewb", [P, CC, T])
        rwb = sb("rwb", [P, C])
        rwst = sb("rwst", [P, 8])
        rbb = sb("rbb", [P, 1])
        mhalf = sb("mhalf", [P, 2 * TJ])
        zero_col = sb("zero_col", [P, 1])
        tick = sb("tick", [P, 1])
        lnbias = sb("lnbias", [P, 2])
        MEAN, VAR, DOT, VE, VN, S1, S2 = range(7)
        stats_all = sb("stats_all", [P, B, TJ, 7])
        weights = sb("weights", [P, TJ * B])
        tokval = sb("tokval", [P, B, TJ, 2])
        ptok = sb("ptok", [P, MB, TJ], i32)

        ARENA = 29400
        arena = sb("arena", [P, ARENA])
        top = [0]

        def place(*shape):
            n = 1
            for s in shape:
                n *= s
            a = arena[:, top[0]:top[0] + n]
            top[0] += n
            assert top[0] <= ARENA, top[0]
            if len(shape) == 2:
                a = a.rearrange("p (a b) -> p a b", b=shape[1])
            elif len(shape) == 3:
                a = a.rearrange("p (a b c) -> p a b c", b=shape[1], c=shape[2])
            return a

        def both(*shape):
            return [place(*shape), place(*shape)]

        xs = [place(T) for _ in range(4)]
        xc = [place(CC, T) for _ in range(4)]
        xm = both(3, T)
        xt = [place(TJ, C) for _ in range(RING)]
        ek = both(CC, T)
        er = both(CC, T)
        ekv = place(CC, T)
        ab = both(2 * CC, T)
        aa = [x[:, 0:CC, :] for x in ab]
        bb = [x[:, CC:2 * CC, :] for x in ab]
        ld = both(CC, T)
        gg = both(CC, T)
        junk = place(TJ, C)
        diff = place(T)
        st6 = both(TJ, 6)
        stat = both(TJ, 7)
        nm = both(TJ)

        ps = ctx.enter_context(nc.psum_tensor("ps", [P, 8, 512], fp32))
        half_top = [0]
        halves = sb("halves", [P, 14336], mybir.dt.float32r)

        def place_half(a, b):
            piece = halves[:, half_top[0]:half_top[0] + a * b].rearrange("p (a b) -> p a b", b=b)
            half_top[0] += a * b
            return piece

        wup_hi, wup_lo = place_half(CC, F), place_half(CC, F)
        oh = halves[:, half_top[0]:half_top[0] + NP * TJ * P].rearrange("p (n j k) -> p n j k", j=TJ, k=P)
        oh32 = oh.bitcast(fp32)
        tok_halves = halves[:, half_top[0] + NP * TJ * P:half_top[0] + NP * TJ * P + B * TJ * 4].rearrange("p (b j a) -> p b j a", j=TJ, a=4)
        wdn_hi, wdn_lo = place_half(FC, C), place_half(FC, C)
        h2_hi, h2_lo = ([place_half(CC, GP * P), place_half(CC, GP * P)] for _ in range(2))
        u_hi, u_lo = place_half(FC, GP * P), place_half(FC, GP * P)
        psK, psR, psV = ps[:, 0:2, :], ps[:, 2:4, :], ps[:, 4:6, :]
        psY = ps[:, 6:8, :].rearrange("p a (j c) -> p (a j) c", c=C)

        wseq = [sb("wseq0", [B, T]), sb("wseq1", [B, T])]
        topv = sb("topv", [B, K])
        topi = sb("topi", [B, K], u32)
        topf = sb("topf", [B, K])
        ones = sb("ones", [B, P])
        slots4 = sb("slots4", [B, 4, K])
        bcol = sb("bcol", [P, 3])
        bcol_i = sb("bcol_i", [P, 1], i32)
        sel = sb("sel", [P, 4, NP])
        row_i = sb("row_i", [P, NP], i32)
        msk_i = sb("msk_i", [P, NP], i32)
        slot_halves = sb("slot_halves", [P, NP, 4])
        slotval = sb("slotval", [P, NP, 2])
        inv = sb("inv", [P, HD // 2])
        ang = sb("ang", [P, NP * HD // 2])
        trn = sb("trn", [P, 2, NP * HD // 2])
        trg = sb("trg", [P, 2, NP, HD // 2])
        blk = sb("blk", [P, P // HD])
        bm = sb("bm", [P, 2])
        tcol = sb("tcol", [P, TJ])
        ssq = sb("ssq", [P, NP])
        rstd = sb("rstd", [P, NP])
        norm2 = [sb("norm2_0", [P, 3]), sb("norm2_1", [P, 3])]
        fst = sb("fst", [P, 2, GP, 10])
        dtick = sb("dtick", [P, 1])

        top[0] = 0
        xsel = place(NP, C)
        x1 = place(NP, C)
        mall = place(NP, K)
        after_mall = top[0]
        ib = place(NP, 2 * K)
        mrow = [place(T) for _ in range(RING)]
        mrt = both(TJ, P)
        squares = both(C)
        spread = place(4, 512)
        FILLED_AHEAD = 2 * H * K + RING * H * 34
        assert top[0] <= ARENA - FILLED_AHEAD
        top[0] = ARENA - FILLED_AHEAD
        pr = both(H, K)
        vblk = [place(2, H // 2 * 34) for _ in range(RING)]
        top[0] = after_mall
        h2T = place(CC, NP * P)
        hn2 = both(C)
        squares2 = both(C)
        after_kept = top[0]
        hn = both(C)
        hnT = both(CC, P)
        rq = both(2 * C)
        rtmp = place(2 * C)
        qT = both(CC, P)
        kblk = [place(CC, 2 * P) for _ in range(2)]
        sc = place(H, K)
        mx = both(H)
        pT = both(H // 2, P)
        rd = both(H)
        osb = both(C)
        oT = both(CC, P)
        w_stage = place(2048)
        assert top[0] <= ARENA - FILLED_AHEAD, top[0]
        top[0] = after_kept
        uT = both(FC, GP * P)
        x2 = both(GP, C)
        share = both(GP, C)
        outr = place(NP, C)

        chan_in = [sem(f"chan_in{p}") for p in range(4)]
        tok_in = [sem(f"tok_in{p}") for p in range(4)]
        row_out = [sem(f"row_out{p}") for p in range(4)]
        w_in = sem("w_in")
        w2_in = sem("w2_in")
        small_in = sem("small_in")
        edges_zero = sem("edges_zero")
        ident_made = sem("ident_made")
        consts_made = sem("consts_made")
        eu_made = sem("eu_made")
        ewb_made = sem("ewb_made")
        rw_chain = sem("rw_chain")
        diff_made = sem("diff_made")
        scaled = sem("scaled")
        mixed = sem("mixed")
        k_ready = sem("k_ready")
        v_ready = sem("v_ready")
        r_ready = sem("r_ready")
        y_ready = sem("y_ready")
        ek_done = sem("ek_done")
        er_done = sem("er_done")
        clamp_done = sem("clamp_done")
        ls_done = sem("ls_done")
        ld_done = sem("ld_done")
        sum_done = sem("sum_done")
        rec_done = sem("rec_done")
        ekv_done = sem("ekv_done")
        scan_done = sem("scan_done")
        den_done = sem("den_done")
        num_done = sem("num_done")
        g_ready = sem("g_ready")
        y_added = sem("y_added")
        bn_done = sem("bn_done")
        aggr_done = sem("aggr_done")
        t2_done = sem("t2_done")
        s2_done = sem("s2_done")
        nm_done = sem("nm_done")
        rows_done = sem("rows_done")
        sel_made = sem("sel_made")
        values_kept = sem("values_kept")
        values_picked = sem("values_picked")
        ib_copied = sem("ib_copied")
        ib_ready = sem("ib_ready")
        idx_turned = sem("idx_turned")
        idx_listed = sem("idx_listed")
        pos_in = sem("pos_in")
        rope_part = sem("rope_part")
        dve_chain = sem("dve_chain")
        stats_kept = sem("stats_kept")
        w_ready = sem("w_ready")
        w_turned = sem("w_turned")
        slots_ready = sem("slots_ready")
        slots_turned = sem("slots_turned")
        idx_ready = sem("idx_ready")
        b_iota = sem("b_iota")
        b_made = sem("b_made")
        blk_made = sem("blk_made")
        bm_made = sem("bm_made")
        inv_made = sem("inv_made")
        ang_ready = sem("ang_ready")
        sin_done = sem("sin_done")
        x_made = sem("x_made")
        ssq_done = sem("ssq_done")
        rstd_done = sem("rstd_done")
        oh_made = sem("oh_made")
        mt_turned = sem("mt_turned")
        mt_copied = sem("mt_copied")
        mask_picked = sem("mask_picked")
        mall_done = sem("mall_done")
        zeros_made = sem("zeros_made")
        spread_made = sem("spread_made")
        hn_made = sem("hn_made")
        hn_turned = sem("hn_turned")
        hnT_done = sem("hnT_done")
        qk_ready = sem("qk_ready")
        v_projected = sem("v_projected")
        rope_done = sem("rope_done")
        vblk_done = sem("vblk_done")
        qk_turned = sem("qk_turned")
        qT_done = sem("qT_done")
        kblk_done = sem("kblk_done")
        scores_ready = sem("scores_ready")
        s_done = sem("s_done")
        mx_done = sem("mx_done")
        sub_done = sem("sub_done")
        exp_done = sem("exp_done")
        p_turned = sem("p_turned")
        pT_done = sem("pT_done")
        pv_ready = sem("pv_ready")
        rd_done = sem("rd_done")
        o_done = sem("o_done")
        o_turned = sem("o_turned")
        oT_done = sem("oT_done")
        o_projected = sem("o_projected")
        x1_done = sem("x1_done")
        w_staged = sem("w_staged")
        w_split = sem("w_split")
        w_rounded = sem("w_rounded")
        h2_rounded = sem("h2_rounded")
        h2_split = sem("h2_split")
        u_rounded = sem("u_rounded")
        u_split = sem("u_split")
        ssq2_done = sem("ssq2_done")
        ln2_done = sem("ln2_done")
        rstd2_done = sem("rstd2_done")
        hn2_made = sem("hn2_made")
        hn2_turned = sem("hn2_turned")
        h2T_done = sem("h2T_done")
        up_ready = sem("up_ready")
        gelu_done = sem("gelu_done")
        down_ready = sem("down_ready")
        x2_done = sem("x2_done")
        x2_read = sem("x2_read")
        x2_weighted = sem("x2_weighted")
        x2_bn_done = sem("x2_bn_done")
        x2_aggr_done = sem("x2_aggr_done")
        x2_var_ready = sem("x2_var_ready")
        x2_pow_done = sem("x2_pow_done")
        outr_ready = sem("outr_ready")
        scattered = sem("scattered")
        rows_in = sem("rows_in")
        mrow_in = [sem(f"mrow_in{k}") for k in range(4)]

        chan_v = x_chan.rearrange("b (c p) t -> b p c t", p=P)
        tok_v = x_tok.rearrange("b (p j) c -> b p j c", j=TJ)
        out_v = out.rearrange("b (p j) c -> b p j c", j=TJ)

        out_rows = out.rearrange("b t c -> (b t) c")

        def rstd_of(tile, at):
            return tile[:, at.n:at.n + 1] if isinstance(at.n, int) else tile[:, bass.ts(at.n, 1)]

        def pair_at(g, i):
            return slice(GP * g.n + i, GP * g.n + i + 1) if isinstance(g.n, int) else bass.ds(g.n * GP + i, 1)

        def first_part_over(eng):
            for k in range(RING):
                eng.wait_ge(row_out[k], 16 * (B // RING))

        block = ctx.enter_context(nc.Block())

        DEPTH = 3

        def periods(eng, period):
            for k in range(RING):
                period(At(0, k))
            with eng.Fori(1, B // RING) as i:
                for k in range(RING):
                    period(At(i, k))
            for k in range(DEPTH):
                period(At(B // RING, k))

        class At:

            def __init__(self, i, k, ring=RING):
                self.i, self.k, self.ring = i + k // ring, k % ring, ring
                self.n = self.i * ring + self.k
                self.par, self.turn = self.k % 2, self.i * (ring // 2) + self.k // 2

            def back(self, d):
                return At(self.i, self.k - d, self.ring)

            def exists(self):
                return not isinstance(self.n, int) or 0 <= self.n < B

            def below(self, count):
                return not isinstance(self.n, int) or self.n < count

            def is_pair(self, back):
                return not isinstance(self.n, int) or 0 <= self.n - back < NP

            def had(self, d):
                return not isinstance(self.n, int) or self.n >= d

        def pairs(eng, period):
            for k in range(RING):
                period(At(0, k))
            with eng.Fori(1, NP // RING - 1) as i:
                for k in range(RING):
                    period(At(i, k))
            for k in range(RING + 4):
                period(At(NP // RING - 1, k))

        def by_twos(eng, count, step):
            for k in range(2):
                step(At(0, k, 2))
            with eng.Fori(1, count // 2 - 1) as i:
                for k in range(2):
                    step(At(i, k, 2))
            for k in range(2):
                step(At(count // 2 - 1, k, 2))

        def ahead(eng, period):
            for k in range(RING):
                period(At(0, k))
            with eng.Fori(1, NP // RING - 1) as i:
                for k in range(RING):
                    period(At(i, k))
            for k in range(RING):
                period(At(NP // RING - 1, k))

        def plain(eng, step):
            for k in range(RING):
                step(At(0, k))
            with eng.Fori(1, NP // RING) as i:
                for k in range(RING):
                    step(At(i, k))

        @block.sync
        def _(sp):
            sp.dma_start(cols[:, :], columns).then_inc(small_in, 16)
            sp.dma_start(rwb[:, :], router_w.rearrange("(a c) -> a c", a=1).to_broadcast([P, C])).then_inc(small_in, 16)
            sp.dma_start(ptok[:, :, :], positions.rearrange("(b t) a -> b (t a)", b=MB)[:, 0:T].rearrange("b (p j) -> p b j", j=TJ)).then_inc(pos_in, 16)
            sp.dma_start(rbb[:, :], router_b.rearrange("(a c) -> a c", a=1).to_broadcast([P, 1])).then_inc(small_in, 16)

            def load_channels(s):
                if s.had(RING):
                    sp.wait_ge(r_ready, s.n - (RING - 1))
                else:
                    sp.wait_ge(edges_zero, 2 * RING)
                sp.dma_start(xs[s.k][0:HALF, 1:T], x_chan[s.n, 0:HALF, 0:T - 1]).then_inc(chan_in[s.k], 16)
                sp.dma_start(xs[s.k][HALF:P, 0:T - 1], x_chan[s.n, HALF:P, 1:T]).then_inc(chan_in[s.k], 16)
                sp.dma_start(xc[s.k][:, :, :], chan_v[s.n]).then_inc(chan_in[s.k], 16)

            def load_tokens(s):
                if s.had(RING):
                    sp.wait_ge(row_out[s.k], 16 * s.i)
                sp.dma_start(xt[s.k][:, :, :], tok_v[s.n]).then_inc(tok_in[s.k], 16)

            def period(at):
                if at.back(-2).exists():
                    load_channels(at.back(-2))
                if at.exists():
                    load_tokens(at)

            load_channels(At(0, 0))
            sp.dma_start(wa[:, :, :, :], w_attn.rearrange("m (c p) o -> p m c o", p=P)).then_inc(w_in, 16)
            load_channels(At(0, 1))
            for k in range(RING):
                period(At(0, k))
            for dst, src in ((wqk, w_qk), (wv, w_v), (wo, w_o)):
                sp.dma_start(dst[:, :, :], src.rearrange("(c p) o -> p c o", p=P)).then_inc(w2_in, 16)
            with sp.Fori(1, B // RING - 1) as i:
                for k in range(RING):
                    period(At(i, k))
            for k in range(RING):
                period(At(B // RING - 1, k))
            sp.wait_ge(mall_done, NP)
            sp.wait_ge(ssq_done, NP)
            sp.dma_start(w_stage.rearrange("p (c o) -> p c o", o=F), w_up.rearrange("(c p) o -> p c o", p=P)).then_inc(w_staged, 16)
            sp.wait_ge(w_split, 1)
            sp.dma_start(w_stage.rearrange("p (c o) -> p c o", o=C), w_down.rearrange("(c p) o -> p c o", p=P)).then_inc(w_staged, 16)

        @block.gpsimd
        def _(pool):
            g = nc.gpsimd
            g.memset(ident[:, :], 0.0).then_inc(ident_made, 1)
            pool.wait_ge(ident_made, 1)
            g.affine_select(out=ident[:, :], in_=ident[:, :], compare_op=ALU.not_equal, fill=1.0,
                            base=0, pattern=[[-1, P]], channel_multiplier=1).then_inc(ident_made, 1)
            g.memset(mhalf[:, :], -0.5).then_inc(consts_made, 1)
            g.memset(zero_col[:, :], 0.0).then_inc(consts_made, 1)
            g.memset(ones[:, :], 1.0).then_inc(consts_made, 1)
            g.memset(lnbias[:, 0:1], -DEN_EXP * LN2).then_inc(consts_made, 1)
            g.memset(lnbias[:, 1:2], 1e-6).then_inc(consts_made, 1)
            g.iota(bcol_i[:, :], pattern=[[0, 1]], base=0, channel_multiplier=1).then_inc(b_iota, 1)
            for d in range(HD // 2):
                g.memset(inv[:, d:d + 1], float(1.0 / np.float32(10000.0) ** np.float32(2.0 * d / HD))).then_inc(inv_made, 1)
            g.memset(blk[:, :], 0.25).then_inc(blk_made, 1)
            pool.wait_ge(blk_made, 1)
            g.affine_select(out=blk[:, :], in_=blk[:, :], compare_op=ALU.is_ge, fill=0.0, base=0,
                            pattern=[[-HD, P // HD]], channel_multiplier=1).then_inc(blk_made, 1)
            pool.wait_ge(blk_made, 2)
            g.affine_select(out=blk[:, :], in_=blk[:, :], compare_op=ALU.is_ge, fill=0.0, base=HD - 1,
                            pattern=[[HD, P // HD]], channel_multiplier=-1).then_inc(blk_made, 1)
            pool.wait_ge(consts_made, 5)
            pool.wait_ge(small_in, 3 * 16)

            def wait_apart(semaphore, value):
                pool.wait_ge(semaphore, value)
                if not isinstance(value, int):
                    g.tensor_tensor(tick[:, :], mhalf[:, 0:1], zero_col[:, :], ALU.add)

            def differences_of(s):
                pool.wait_ge(chan_in[s.k], 48 * (s.i + 1))
                if s.had(2):
                    pool.wait_ge(r_ready, s.n - 1)
                g.tensor_tensor(diff[:, :], xc[s.k][:, 0, :], xs[s.k][:, :], ALU.subtract).then_inc(diff_made, 1)
                wait_apart(diff_made, s.n + 1)
                for m in range(3):
                    last = g.tensor_scalar(xm[s.par][:, m, :], diff[:, :], mix[:, m:m + 1], 0.0, ALU.mult, ALU.add)
                last.then_inc(scaled, 1)

            def mixes_of(s):
                pool.wait_ge(scaled, s.n + 1)
                for m in range(3):
                    last = g.tensor_tensor(xm[s.par][:, m, :], xm[s.par][:, m, :], xs[s.k][:, :], ALU.add)
                last.then_inc(mixed, 1)

            def log_sum_of(s):
                pool.wait_ge(ls_done, s.n + 1)
                g.tensor_tensor(ld[s.par][:, :, :], ld[s.par][:, :, :], er[s.par][:, :, :], ALU.add).then_inc(sum_done, 1)

            def scale_of(s):
                pool.wait_ge(t2_done, s.n + 1)
                if s.had(2):
                    pool.wait_ge(rows_done, s.n)
                g.tensor_tensor(stat[s.par][:, :, S1:S2 + 1], stat[s.par][:, :, VE:VN + 1], mhalf[:, 0:2 * TJ].rearrange("p (j a) -> p j a", a=2), ALU.pow).then_inc(s2_done, 1)

            pool.wait_ge(mixed, 1)

            def period(at):
                nxt = at.back(-1)
                if nxt.exists():
                    differences_of(nxt)
                    mixes_of(nxt)
                if at.had(1) and at.back(1).exists():
                    log_sum_of(at.back(1))
                if at.had(3) and at.back(3).exists():
                    scale_of(at.back(3))

            for k in range(RING):
                period(At(0, k))
            with pool.Fori(1, B // RING - 1) as i:
                for k in range(RING):
                    period(At(i, k))
            for k in range(RING + DEPTH):
                period(At(B // RING - 1, k))

            def store_group(n):
                pool.wait_ge(outr_ready, n + 1)
                for q in range(GP * n, GP * (n + 1)):
                    g.indirect_dma_start(out_rows, bass.IndirectOffsetOnAxis(ap=row_i[:, q:q + 1], axis=0),
                                         outr[:, q, :], None).then_inc(scattered, 16)

            pool.wait_ge(idx_ready, 2)
            first_part_over(pool)
            for q in range(NP):
                g.indirect_dma_start(xsel[:, q, :], None, out_rows,
                                     bass.IndirectOffsetOnAxis(ap=row_i[:, q:q + 1], axis=0)).then_inc(rows_in, 16)
            for q in range(NP):
                if q >= RING:
                    pool.wait_ge(mt_turned, q - RING + 1)
                g.indirect_dma_start(mrow[q % RING], None, mask_rows,
                                     bass.IndirectOffsetOnAxis(ap=msk_i[:, q:q + 1], axis=0)).then_inc(mrow_in[q % RING], 16)
            for n, (hi, lo) in enumerate(((wup_hi, wup_lo), (wdn_hi, wdn_lo))):
                pool.wait_ge(w_staged, 16 * (n + 1))
                g.tensor_copy(hi.rearrange("p c o -> p (c o)"), w_stage).then_inc(w_rounded, 1)
                pool.wait_ge(w_rounded, n + 1)
                g.tensor_tensor(lo.rearrange("p c o -> p (c o)"), w_stage, hi.rearrange("p c o -> p (c o)").bitcast(fp32), ALU.subtract).then_inc(w_split, 1)
            for group in range(NG):
                pool.wait_ge(x2_var_ready, group + 1)
                g.tensor_tensor(fst[:, group % 2, :, 9], fst[:, group % 2, :, 8], mhalf[:, 0:GP], ALU.pow).then_inc(x2_pow_done, 1)
                if group >= 1:
                    store_group(group - 1)
            store_group(NG - 1)
            pool.wait_ge(scattered, 16 * NP)

        @block.tensor
        def _(pe):
            mm = nc.tensor.matmul

            def keep_warm(bank, count):
                for _ in range(count):
                    mm(ps[:, bank, 0:P], ident[:, :], ident[:, :], start=True, stop=True)

            def projections(s):
                pe.wait_ge(mixed, s.n + 1)
                for m, ps, ready, used in ((0, psK, k_ready, ek_done), (1, psV, v_ready, ekv_done), (2, psR, r_ready, er_done)):
                    if s.had(1):
                        pe.wait_ge(used, s.n)
                    for o in range(CC):
                        for c in range(CC):
                            rhs = xm[s.par][:, m, :] if c == 0 else xc[s.k][:, c, :]
                            last = mm(ps[:, o, :], wa[:, m, c, o * P:(o + 1) * P], rhs, start=(c == 0), stop=(c == CC - 1))
                    last.then_inc(ready, 1)

            def outputs(s):
                pe.wait_ge(g_ready, s.n + 1)
                if s.had(1):
                    pe.wait_ge(y_added, s.n)
                for j in range(TJ):
                    for c in range(CC):
                        last = mm(psY[:, j, :], gg[s.par][:, c, j * P:(j + 1) * P], wa[:, 3, c, :], start=(c == 0), stop=(c == CC - 1))
                last.then_inc(y_ready, 1)

            def period(at):
                if at.exists():
                    projections(at)
                if isinstance(at.n, int) and at.n >= B + 1:
                    pe.wait_ge(ek_done, B)
                    keep_warm(0, 14)
                if at.had(2) and at.back(2).exists():
                    outputs(at.back(2))

            pe.wait_ge(ident_made, 2)
            keep_warm(7, 18)
            pe.wait_ge(w_in, 16)
            periods(pe, period)

            pe.wait_ge(w_ready, 1)
            pe.wait_ge(ident_made, 2)
            pe.wait_ge(consts_made, 5)
            pe.wait_ge(y_added, B)
            for j in range(TJ):
                last = nc.tensor.transpose(ps[0:B, 7, j * P:(j + 1) * P], weights[:, j * B:(j + 1) * B], ident[:, :])
            last.then_inc(w_turned, 1)

            def slots_turn(i):
                for h in range(2):
                    last = mm(ps[h * K:(h + 1) * K, 5 + i // 2, i * NP:(i + 1) * NP], slots4[:, i, :], ident[0:B, h:B:2], start=True, stop=True)
                return last

            pe.wait_ge(idx_listed, 1)
            slots_turn(0)
            slots_turn(1).then_inc(idx_turned, 1)
            for i in range(4):
                pe.wait_ge(spread_made, i + 1)
                mm(ps[:, i, :], ones[:, :], spread[0:B, i, :], start=True, stop=True).then_inc(ib_ready, 1)
            pe.wait_ge(slots_ready, 1)
            slots_turn(2)
            slots_turn(3).then_inc(slots_turned, 1)

            def pick_values(at):
                pe.wait_ge(oh_made, at.n + 1)
                if at.had(2):
                    pe.wait_ge(values_kept, at.n - 1)
                for j in range(TJ):
                    last = mm(ps[:, 6 + at.par, 0:8], oh[:, at.n, j, :], tok_halves[:, 2 * at.n:2 * at.n + 2, j, :],
                              start=(j == 0), stop=(j == TJ - 1))
                last.then_inc(values_picked, 1)

            def mask_turn(at):
                pe.wait_ge(mrow_in[at.k], 16 * (at.i + 1))
                if at.had(2):
                    pe.wait_ge(mt_copied, at.n - 1)
                for j in range(TJ):
                    last = nc.tensor.transpose(ps[:, at.par, j * P:(j + 1) * P],
                                               mrow[at.k].rearrange("p (q j) -> p j q", j=TJ)[:, j, :], ident[:, :])
                last.then_inc(mt_turned, 1)

            def mask_pick(at):
                pe.wait_ge(mt_copied, at.n + 1)
                if at.had(2):
                    pe.wait_ge(mall_done, at.n - 1)
                for j in range(TJ):
                    last = mm(ps[:, 2 + at.par, 0:P], mrt[at.par][:, j, :], oh32[:, at.n, j, :], start=(j == 0), stop=(j == TJ - 1))
                last.then_inc(mask_picked, 1)

            for q in range(NP):
                pick_values(At(q // RING, q % RING))
            pe.wait_ge(ib_copied, 4)
            mask_turn(At(0, 0))

            def mask_period(at):
                if at.back(-1).below(NP):
                    mask_turn(at.back(-1))
                mask_pick(at)

            ahead(pe, mask_period)

            def project_qk(at):
                pe.wait_ge(hnT_done, at.n + 1)
                if at.had(1):
                    pe.wait_ge(rope_done, at.n)
                for c in range(CC):
                    last = mm(ps[:, 7, :], hnT[at.par][:, c, :], wqk[:, c, :], start=(c == 0), stop=(c == CC - 1))
                last.then_inc(qk_ready, 1)

            def project_v(at):
                if at.had(3):
                    pe.wait_ge(o_done, at.n - 2)
                for c in range(CC):
                    last = mm(ps[:, 4, 0:C], hnT[at.par][:, c, :], wv[:, c, :], start=(c == 0), stop=(c == CC - 1))
                last.then_inc(v_projected, 1)

            def p_turn(at):
                pe.wait_ge(exp_done, at.n + 1)
                for t in range(4):
                    for c in range(CC):
                        last = nc.tensor.transpose(ps[:, t // 2, (t % 2 * CC + c) * P:(t % 2 * CC + c + 1) * P],
                                                   pr[at.par].rearrange("p h k -> p (h k)")[:, (t * CC + c) * P:(t * CC + c + 1) * P], ident[:, :])
                last.then_inc(p_turned, 1)

            def o_turn(at):
                pe.wait_ge(o_done, at.n + 1)
                if at.had(1):
                    pe.wait_ge(x1_done, at.n)
                for c in range(CC):
                    last = nc.tensor.transpose(ps[:, 6, c * P:(c + 1) * P], osb[at.par][:, c * P:(c + 1) * P], ident[:, :])
                last.then_inc(o_turned, 1)

            def hn_turn(at):
                pe.wait_ge(hn_made, at.n + 1)
                if at.had(2):
                    pe.wait_ge(qT_done, at.n - 1)
                    pe.wait_ge(kblk_done, at.n - 1)
                for c in range(CC):
                    last = nc.tensor.transpose(ps[:, 5, c * P:(c + 1) * P], hn[at.par][:, c * P:(c + 1) * P], ident[:, :])
                last.then_inc(hn_turned, 1)

            def scores(at):
                pe.wait_ge(qT_done, at.n + 1)
                pe.wait_ge(kblk_done, at.n + 1)
                if at.had(1):
                    pe.wait_ge(pT_done, at.n)
                for b in range(2):
                    for c in range(CC):
                        for t in range(4):
                            rows = slice(32 * t, 32 * t + 32)
                            keys = kblk[at.par][rows, c, :].rearrange("p (h k) -> p h k", h=2)
                            last = mm(ps[b * K:(b + 1) * K, t, c * P:(c + 1) * P].rearrange("p (h k) -> p h k", h=2),
                                      qT[at.par][rows, c, b * K:(b + 1) * K], keys[:, :, b * K:(b + 1) * K], start=True, stop=True)
                last.then_inc(scores_ready, 1)

            def qk_turn(at, hn_before):
                pe.wait_ge(rope_done, at.n + 1)
                pe.wait_ge(hnT_done, hn_before)
                for c in range(4):
                    last = nc.tensor.transpose(ps[:, 5, c * P:(c + 1) * P], rq[at.par][:, c * P:(c + 1) * P], ident[:, :])
                last.then_inc(qk_turned, 1)

            def values(at, v_before):
                pe.wait_ge(pT_done, at.n + 1)
                pe.wait_ge(vblk_done, v_before)
                for b in range(2):
                    for hp in range(H // 2):
                        last = mm(ps[b * K:(b + 1) * K, 4, hp * 34:(hp + 1) * 34], pT[at.par][:, hp % 4 * CC + hp // 4, b * K:(b + 1) * K],
                                  vblk[at.k][:, b, hp * 34:(hp + 1) * 34], start=True, stop=True)
                last.then_inc(pv_ready, 1)

            def project_o(at):
                pe.wait_ge(oT_done, at.n + 1)
                for c in range(CC):
                    last = mm(ps[:, 6, 0:C], oT[at.par][:, c, :], wo[:, c, :], start=(c == 0), stop=(c == CC - 1))
                last.then_inc(o_projected, 1)

            def hn2_turn(at, q_before):
                pe.wait_ge(hn2_made, at.n + 1)
                pe.wait_ge(rope_done, q_before)
                for c in range(CC):
                    last = nc.tensor.transpose(ps[:, 7, c * P:(c + 1) * P], hn2[at.par][:, c * P:(c + 1) * P], ident[:, :])
                last.then_inc(hn2_turned, 1)

            def att_period(at):
                if at.below(NP):
                    project_qk(at)
                if at.is_pair(2):
                    p_turn(at.back(2))
                if at.below(NP):
                    project_v(at)
                if at.is_pair(3):
                    o_turn(at.back(3))
                if at.back(-1).below(NP):
                    hn_turn(at.back(-1))
                if isinstance(at.n, int) and (at.n < 2 or at.n > NP):
                    keep_warm(3, 10)
                if at.is_pair(1):
                    scores(at.back(1))
                if at.below(NP):
                    qk_turn(at, at.n + 2 if at.back(-1).below(NP) else NP)
                if at.is_pair(4):
                    hn2_turn(at.back(4), at.n + 1 if at.below(NP) else NP)
                if at.is_pair(2):
                    values(at.back(2), at.n + 1 if at.below(NP) else NP)
                if at.is_pair(4):
                    pe.wait_ge(h2T_done, at.back(4).n + 1)
                if at.is_pair(3):
                    project_o(at.back(3))

            pe.wait_ge(w2_in, 3 * 16)
            hn_turn(At(0, 0))
            pairs(pe, att_period)

            def up(g):
                pe.wait_ge(h2_split, g.n + 1)
                for k in range(FC // 2):
                    if g.had(1):
                        pe.wait_ge(gelu_done, FC // 2 * (g.n - 1) + k + 1)
                    for h in range(2):
                        chunk = slice((2 * k + h) * P, (2 * k + h + 1) * P)
                        for c in range(CC):
                            for t, (w, x) in enumerate(((wup_hi, h2_hi), (wup_hi, h2_lo), (wup_lo, h2_hi))):
                                last = mm(ps[:, k, h * GP * P:(h + 1) * GP * P], w[:, c, chunk], x[g.par][:, c, :],
                                          start=(c == 0 and t == 0), stop=(c == CC - 1 and t == 2))
                    last.then_inc(up_ready, 1)

            def down(g):
                pe.wait_ge(u_split, g.n + 1)
                if g.had(2):
                    pe.wait_ge(x2_read, g.n - 1)
                for i in range(GP):
                    for f in range(FC):
                        for t, (x, w) in enumerate(((u_hi, wdn_hi), (u_hi, wdn_lo), (u_lo, wdn_hi))):
                            last = mm(ps[:, 4 + g.par, i * C:(i + 1) * C], x[:, f, i * P:(i + 1) * P], w[:, f, :],
                                      start=(f == 0 and t == 0), stop=(f == FC - 1 and t == 2))
                last.then_inc(down_ready, 1)

            def mlp_period(g):
                if g.back(-1).below(NG):
                    up(g.back(-1))
                down(g)

            pe.wait_ge(w_split, 2)
            up(At(0, 0, 2))
            by_twos(pe, NG, mlp_period)

        @block.scalar
        def _(act):
            a = nc.scalar
            a.preload_act_table_set("natural_log_exp_and_others")
            act.wait_ge(small_in, 3 * 16)
            a.activation(euw[:, :, :], uw, ACT.Exp, scale=1.0 / T).then_inc(eu_made, 1)
            act.wait_ge(consts_made, 5)

            def exp_k_of(s):
                act.wait_ge(k_ready, s.n + 1)
                if s.had(2):
                    act.wait_ge(den_done, s.n - 1)
                a.activation(ek[s.par][:, :, :], psK[:, :, :], ACT.Exp).then_inc(ek_done, 1)

            def exp_r_of(s):
                act.wait_ge(r_ready, s.n + 1)
                if s.had(2):
                    act.wait_ge(sum_done, s.n - 1)
                a.activation(er[s.par][:, :, :], psR[:, :, :], ACT.Exp, scale=-1.0).then_inc(er_done, 1)

            def ln_den_of(s):
                act.wait_ge(den_done, s.n + 1)
                if s.had(2):
                    act.wait_ge(g_ready, s.n - 1)
                a.activation(ld[s.par][:, :, :], bb[s.par][:, :, :], ACT.Ln, scale=2.0 ** -DEN_EXP).then_inc(ld_done, 1)

            def ln_gate_of(s):
                act.wait_ge(clamp_done, s.n + 1)
                a.activation(er[s.par][:, :, :], er[s.par][:, :, :], ACT.Ln, bias=1.0).then_inc(ls_done, 1)

            def reciprocal_of(s):
                act.wait_ge(sum_done, s.n + 1)
                a.activation(ld[s.par][:, :, :], ld[s.par][:, :, :], ACT.Exp, scale=-1.0, bias=lnbias[:, 0:1]).then_inc(rec_done, 1)

            def rows_of(s):
                act.wait_ge(nm_done, s.n + 1)
                for j in range(TJ):
                    last = a.activation(xt[s.k][:, j, :], xt[s.k][:, j, :], ACT.Identity,
                                        scale=stat[s.par][:, j, S2:S2 + 1], bias=nm[s.par][:, j:j + 1])
                last.then_inc(rows_done, 1)
                act.wait_ge(rows_done, s.n + 1)
                act.dma_start(out_v[s.n], xt[s.k][:, :, :]).then_inc(row_out[s.k], 16)

            def period(at):
                if at.exists():
                    exp_k_of(at)
                if at.had(1) and at.back(1).exists():
                    reciprocal_of(at.back(1))
                if at.exists():
                    exp_r_of(at)
                    ln_den_of(at)
                    ln_gate_of(at)
                if at.had(3) and at.back(3).exists():
                    rows_of(at.back(3))

            periods(act, period)

            first_part_over(act)
            for i in range(4):
                act.wait_ge(ib_ready, i + 1)
                a.activation(ib[:, 4 * i:4 * i + 4, :].rearrange("p n k -> p (n k)"), ps[:, i, :], ACT.Copy).then_inc(ib_copied, 1)

            act.wait_ge(ang_ready, 1)
            a.activation(trg[:, :, :, :].rearrange("p a n d -> p (a n d)"), trn[:, :, :].rearrange("p a n -> p (a n)"), ACT.Sin).then_inc(sin_done, 1)
            a.preload_act_table_set("natural_log_exp_and_others")

            def mask_copy(at):
                act.wait_ge(mt_turned, at.n + 1)
                if at.had(2):
                    act.wait_ge(mask_picked, at.n - 1)
                a.activation(mrt[at.par].rearrange("p c k -> p (c k)"), ps[:, at.par, :], ACT.Copy).then_inc(mt_copied, 1)

            def square_of(at):
                act.wait_ge(x_made, at.n + 1)
                if at.had(2):
                    act.wait_ge(ssq_done, at.n - 1)
                a.activation(squares[at.par], xsel[:, at.n, :], ACT.Square, accum_out=rstd_of(ssq, at)).then_inc(ssq_done, 1)

            def slot_period(at):
                mask_copy(at)
                square_of(at)

            plain(act, slot_period)
            act.wait_ge(ssq_done, NP)
            a.activation(rstd[:, :], ssq[:, :], ACT.Ln, scale=1.0 / C, bias=lnbias[:, 1:2]).then_inc(rstd_done, 1)
            act.wait_ge(rstd_done, 1)
            a.activation(rstd[:, :], rstd[:, :], ACT.Exp, scale=-0.5).then_inc(rstd_done, 1)

            def hnT_copy(at):
                act.wait_ge(hn_turned, at.n + 1)
                if at.had(2):
                    act.wait_ge(v_projected, at.n - 1)
                for c in range(CC):
                    last = a.activation(hnT[at.par][:, c, :], ps[:, 5, c * P:(c + 1) * P], ACT.Copy, scale=gains[:, 0, c:c + 1])
                last.then_inc(hnT_done, 1)

            def v_copy(at):
                act.wait_ge(v_projected, at.n + 1)
                if at.had(RING):
                    act.wait_ge(pv_ready, at.n - RING + 1)
                for b in range(2):
                    for h in range(2):
                        dst = vblk[at.k][h * K:(h + 1) * K, b, :].rearrange("p (n d) -> p n d", d=34)[:, :, h * HD:(h + 1) * HD]
                        src = ps[b * K:(b + 1) * K, 4, 0:C].rearrange("p (n d) -> p n d", d=2 * HD)[:, :, h * HD:(h + 1) * HD]
                        last = a.activation(dst, src, ACT.Copy)
                last.then_inc(vblk_done, 1)

            def exp_p(at):
                act.wait_ge(sub_done, at.n + 1)
                if at.had(2):
                    act.wait_ge(p_turned, at.n - 1)
                a.activation(pr[at.par][:, :, 0:KC], sc[:, :, 0:KC], ACT.Exp).then_inc(exp_done, 1)

            def q_copy(at):
                act.wait_ge(qk_turned, at.n + 1)
                if at.had(2):
                    act.wait_ge(scores_ready, at.n - 1)
                a.activation(qT[at.par].rearrange("p c k -> p (c k)"), ps[:, 5, 0:CC * P], ACT.Copy).then_inc(qT_done, 1)

            def k_copy(at):
                for h in range(2):
                    last = a.activation(kblk[at.par][:, :, h * P:(h + 1) * P], ps[:, 5, CC * P:2 * CC * P].rearrange("p (c k) -> p c k", c=CC),
                                        ACT.Copy, scale=bm[:, h:h + 1])
                last.then_inc(kblk_done, 1)

            def pT_copy(at):
                act.wait_ge(p_turned, at.n + 1)
                if at.had(2):
                    act.wait_ge(pv_ready, at.n - 1)
                a.activation(pT[at.par].rearrange("p n k -> p (n k)"), ps[:, 0:2, :].rearrange("p b k -> p (b k)"), ACT.Copy).then_inc(pT_done, 1)

            def oT_copy(at):
                act.wait_ge(o_turned, at.n + 1)
                a.activation(oT[at.par].rearrange("p c k -> p (c k)"), ps[:, 6, 0:C], ACT.Copy).then_inc(oT_done, 1)

            def norm2_of(at):
                act.wait_ge(x1_done, at.n + 1)
                a.activation(squares2[at.par], x1[:, at.n, :], ACT.Square, accum_out=norm2[at.par][:, 0:1]).then_inc(ssq2_done, 1)
                act.wait_ge(ssq2_done, at.n + 1)
                a.activation(norm2[at.par][:, 1:2], norm2[at.par][:, 0:1], ACT.Ln, scale=1.0 / C, bias=lnbias[:, 1:2]).then_inc(ln2_done, 1)
                act.wait_ge(ln2_done, at.n + 1)
                a.activation(norm2[at.par][:, 2:3], norm2[at.par][:, 1:2], ACT.Exp, scale=-0.5).then_inc(rstd2_done, 1)

            def h2T_copy(at):
                act.wait_ge(hn2_turned, at.n + 1)
                for c in range(CC):
                    last = a.activation(h2T[:, c, bass.ts(at.n, P)], ps[:, 7, c * P:(c + 1) * P], ACT.Copy, scale=gains[:, 1, c:c + 1])
                last.then_inc(h2T_done, 1)

            def att_period(at):
                if at.is_pair(4):
                    norm2_of(at.back(4))
                if at.is_pair(2):
                    pT_copy(at.back(2))
                if at.below(NP):
                    v_copy(at)
                if at.is_pair(3):
                    oT_copy(at.back(3))
                if at.back(-1).below(NP):
                    hnT_copy(at.back(-1))
                if at.below(NP):
                    q_copy(at)
                    k_copy(at)
                if at.is_pair(4):
                    h2T_copy(at.back(4))
                if at.is_pair(1):
                    exp_p(at.back(1))

            hnT_copy(At(0, 0))
            act.wait_ge(bm_made, 1)
            act.wait_ge(zeros_made, 3 * RING + 2)
            pairs(act, att_period)

            a.preload_act_table(ACT.Gelu_apprx_tanh)

            def gelu_of(g):
                if g.had(2):
                    act.wait_ge(u_split, g.n - 1)
                for k in range(FC // 2):
                    act.wait_ge(up_ready, FC // 2 * g.n + k + 1)
                    a.activation(uT[g.par][:, 2 * k:2 * k + 2, :].rearrange("p f n -> p (f n)"), ps[:, k, :], ACT.Gelu_apprx_tanh).then_inc(gelu_done, 1)

            by_twos(act, NG, gelu_of)

        @block.vector
        def _(dve):
            v = nc.vector
            for k in range(RING):
                v.memset(xs[k][0:HALF, 0:1], 0.0).then_inc(edges_zero, 1)
                v.memset(xs[k][HALF:P, T - 1:T], 0.0).then_inc(edges_zero, 1)
            dve.wait_ge(small_in, 3 * 16)
            dve.wait_ge(chan_in[0], 48)
            v.tensor_tensor(diff[:, :], xc[0][:, 0, :], xs[0][:, :], ALU.subtract).then_inc(diff_made, 1)
            dve.wait_ge(diff_made, 1)
            for m, done in enumerate((None, scaled, mixed)):
                last = v.scalar_tensor_tensor(xm[0][:, m, :], diff[:, :], mix[:, m:m + 1], xs[0][:, :], ALU.mult, ALU.add)
                if done is not None:
                    last.then_inc(done, 1)
            v.memset(ewb[:, :, :], 1.0).then_inc(ewb_made, 1)
            dve.wait_ge(ewb_made, 1)
            dve.wait_ge(b_iota, 1)
            v.tensor_copy(bcol[:, 0:1], bcol_i[:, :]).then_inc(b_made, 1)
            dve.wait_ge(b_made, 1)
            v.tensor_scalar(bcol[:, 1:2], bcol[:, 0:1], float(T), None, ALU.mult)
            v.tensor_scalar(bcol[:, 2:3], bcol[:, 0:1], float(MB - 1), float(S // T * S), ALU.min, ALU.mult)
            for j in range(TJ):
                v.tensor_scalar(tcol[:, j:j + 1], bcol[:, 0:1], float(TJ), float(j), ALU.mult, ALU.add)
            dve.wait_ge(pos_in, 16)
            v.tensor_copy(tokval[:, 0:MB, :, 1], ptok[:, :, :])
            v.tensor_copy(tokval[:, MB:B, :, 1], ptok[:, MB - 1, :].unsqueeze(1).to_broadcast([P, B - MB, TJ])).then_inc(b_made, 1)
            dve.wait_ge(b_made, 2)
            dve.wait_ge(eu_made, 1)
            dve.wait_ge(blk_made, 3)
            v.reduce_sum(bm[:, :], blk[:, :].rearrange("p (n h) -> p h n", h=2), AX.X).then_inc(bm_made, 1)
            for c in range(CC):
                v.tensor_scalar(ewb[:, c, :], ewb[:, c, :], euw[:, 1, c:c + 1], None, ALU.mult).then_inc(ewb_made, 1)
            v.bn_stats(rwst[:, 0:6], rwb[:, :]).then_inc(rw_chain, 1)
            dve.wait_ge(rw_chain, 1)
            v.bn_aggr(rwst[:, 6:8], rwst[:, 0:6]).then_inc(rw_chain, 1)
            dve.wait_ge(rw_chain, 2)
            v.tensor_scalar(rwb[:, :], rwb[:, :], rwst[:, 6:7], None, ALU.subtract).then_inc(rw_chain, 1)
            dve.wait_ge(rw_chain, 3)
            dve.wait_ge(ewb_made, 1 + CC)

            def recurrence_of(s):
                par = s.par
                dve.wait_ge(v_ready, s.n + 1)
                dve.wait_ge(ek_done, s.n + 1)
                v.tensor_tensor(ekv[:, :, :], ek[par][:, :, :], psV[:, :, :], ALU.mult).then_inc(ekv_done, 1)
                if s.had(2):
                    dve.wait_ge(ld_done, s.n - 1)
                    dve.wait_ge(g_ready, s.n - 1)
                v.memset(ab[par][:, :, 0:1], 0.0)
                for c in range(CC):
                    v.tensor_tensor_scan(bb[par][:, c, 1:T], ewb[:, c, 0:T - 1], ek[par][:, c, 0:T - 1], 0.0, ALU.mult, ALU.add)
                dve.wait_ge(ekv_done, s.n + 1)
                for c in range(CC):
                    last = v.tensor_tensor_scan(aa[par][:, c, 1:T], ewb[:, c, 0:T - 1], ekv[:, c, 0:T - 1], 0.0, ALU.mult, ALU.add)
                last.then_inc(scan_done, 1)
                dve.wait_ge(scan_done, s.n + 1)
                for c in range(CC):
                    last = v.scalar_tensor_tensor(bb[par][:, c, :], ek[par][:, c, :], euw[:, 0, c:c + 1], bb[par][:, c, :], ALU.mult, ALU.add)
                last.then_inc(den_done, 1)
                for c in range(CC):
                    last = v.scalar_tensor_tensor(aa[par][:, c, :], ekv[:, c, :], euw[:, 0, c:c + 1], aa[par][:, c, :], ALU.mult, ALU.add)
                last.then_inc(num_done, 1)

            def clamp_of(s):
                dve.wait_ge(er_done, s.n + 1)
                v.tensor_scalar(er[s.par][:, :, :], er[s.par][:, :, :], 2.0 ** 62, None, ALU.min).then_inc(clamp_done, 1)

            def gate_of(s):
                par = s.par
                dve.wait_ge(rec_done, s.n + 1)
                if s.had(2):
                    dve.wait_ge(y_ready, s.n - 1)
                dve.wait_ge(num_done, s.n + 1)
                for c in range(CC):
                    last = v.tensor_tensor(gg[par][:, c, :].rearrange("p (j q) -> p q j", j=TJ),
                                           aa[par][:, c, :].rearrange("p (q j) -> p q j", j=TJ),
                                           ld[par][:, c, :].rearrange("p (q j) -> p q j", j=TJ), ALU.mult)
                last.then_inc(g_ready, 1)

            def statistics_of(s):
                par = s.par
                dve.wait_ge(y_ready, s.n + 1)
                dve.wait_ge(tok_in[s.k], 16 * (s.i + 1))
                v.tensor_tensor(xt[s.k][:, :, :], psY[:, :, :], xt[s.k][:, :, :], ALU.add).then_inc(y_added, 1)
                dve.wait_ge(y_added, s.n + 1)
                for j in range(TJ):
                    last = v.bn_stats(st6[par][:, j, :], xt[s.k][:, j, :])
                last.then_inc(bn_done, 1)
                for j in range(TJ):
                    if j == TJ - 1:
                        dve.wait_ge(bn_done, s.n + 1)
                    v.tensor_tensor_reduce(junk[:, j, :], xt[s.k][:, j, :], rwb[:, :], 1.0, 0.0, ALU.mult, ALU.add,
                                           stat[par][:, j, 2:3])
                for j in range(TJ):
                    last = v.bn_aggr(stat[par][:, j, 0:2], st6[par][:, j, :])
                last.then_inc(aggr_done, 1)
                dve.wait_ge(aggr_done, s.n + 1)
                v.tensor_scalar(stat[par][:, :, VE], stat[par][:, :, VAR], EPS, None, ALU.add)
                v.tensor_scalar(stat[par][:, :, VN], stat[par][:, :, VAR], 1.0 + EPS / 4, EPS * EPS / 4, ALU.mult, ALU.add).then_inc(t2_done, 1)

            def shift_of(s):
                dve.wait_ge(s2_done, s.n + 1)
                v.scalar_tensor_tensor(nm[s.par][:, :], stat[s.par][:, :, MEAN], -1.0, stat[s.par][:, :, S2], ALU.mult, ALU.mult).then_inc(nm_done, 1)
                v.tensor_copy(stats_all[:, s.n, :, :], stat[s.par][:, :, :]).then_inc(stats_kept, 1)

            def period(at):
                if at.exists():
                    recurrence_of(at)
                if at.exists():
                    clamp_of(at)
                if at.had(1) and at.back(1).exists():
                    gate_of(at.back(1))
                if at.had(3) and at.back(3).exists():
                    shift_of(at.back(3))
                if at.had(2) and at.back(2).exists():
                    statistics_of(at.back(2))

            periods(dve, period)

            n_chain = [0]

            def link(ins):
                n_chain[0] += 1
                ins.then_inc(dve_chain, 1)
                dve.wait_ge(dve_chain, n_chain[0])

            dve.wait_ge(stats_kept, B)
            link(v.tensor_tensor(weights[:, :].rearrange("p (j b) -> p b j", j=TJ), stats_all[:, :, :, DOT], stats_all[:, :, :, S1], ALU.mult))
            v.tensor_scalar(weights[:, :], weights[:, :], rbb[:, 0:1], None, ALU.add).then_inc(w_ready, 1)
            link(v.tensor_tensor(tokval[:, :, :, 0], stats_all[:, :, :, VN], stats_all[:, :, :, S2], ALU.mult))
            link(v.tensor_tensor(tokval[:, :, :, 0], tokval[:, :, :, 0], stats_all[:, :, :, S1], ALU.mult))
            link(v.tensor_copy(tok_halves[:, :, :, 0:2], tokval[:, :, :, :]))
            v.tensor_tensor(tok_halves[:, :, :, 2:4], tokval[:, :, :, :], tok_halves[:, :, :, 0:2].bitcast(fp32), ALU.subtract)
            dve.wait_ge(w_turned, 1)
            link(v.tensor_copy(wseq[0][:, :].rearrange("b (p j) -> b j p", j=TJ), ps[0:B, 7, :].rearrange("b (j p) -> b j p", j=TJ)))
            for r in range(K // 8):
                eight = slice(8 * r, 8 * r + 8)
                link(v.max(topv[:, eight], wseq[r % 2][:, :]))
                link(v.max_index(topi[:, eight], topv[:, eight], wseq[r % 2][:, :]))
                if r < K // 8 - 1:
                    link(v.match_replace(wseq[1 - r % 2][:, :], topv[:, eight], wseq[r % 2][:, :], NEG))
            link(v.tensor_copy(topf[:, :], topi[:, :]))
            v.tensor_scalar(slots4[:, 0, :], topf[:, :], bcol[0:B, 1:2], None, ALU.add)
            v.tensor_scalar(slots4[:, 1, :], topf[:, :], float(S // T), bcol[0:B, 2:3], ALU.mult, ALU.add).then_inc(idx_listed, 1)
            for i in range(4):
                v.tensor_tensor(spread[0:B, i, :].rearrange("b (n k) -> b n k", k=K), topf[:, :].unsqueeze(1).to_broadcast([B, B // 4, K]),
                                ident[0:B, i * B // 4:(i + 1) * B // 4].unsqueeze(2).to_broadcast([B, B // 4, K]), ALU.mult).then_inc(spread_made, 1)
            dve.wait_ge(idx_turned, 1)
            v.tensor_copy(row_i[:, :], ps[:, 5, 0:NP]).then_inc(idx_ready, 1)
            v.tensor_copy(msk_i[:, :], ps[:, 5, NP:2 * NP]).then_inc(idx_ready, 1)
            link(v.tensor_scalar(slots4[:, 3, :], topv[:, :], topv[:, K - 1:K], -1.0, ALU.is_gt, ALU.mult))
            v.tensor_scalar(slots4[:, 3, :], slots4[:, 3, :], 2.0, None, ALU.add)
            v.tensor_copy(slots4[:, 2, 0:KC], topv[:, 0:KC])
            v.memset(slots4[:, 2, KC:K], 0.0).then_inc(slots_ready, 1)
            first_part_over(dve)
            for k in range(RING):
                v.memset(vblk[k], 0.0).then_inc(zeros_made, 1)
            for par in range(2):
                v.memset(pr[par][:, :, KC:K], 0.0).then_inc(zeros_made, 1)
            dve.wait_ge(zeros_made, RING + 2)
            for k in range(RING):
                for h in range(2):
                    v.memset(vblk[k][h * K:(h + 1) * K, :, :].rearrange("p b (n d) -> p (b n) d", d=34)[:, :, 32 + h:33 + h], 1.0).then_inc(zeros_made, 1)
            dve.wait_ge(slots_turned, 1)
            v.tensor_copy(sel[:, 2:4, :].rearrange("p a n -> p (a n)"), ps[:, 6, 2 * NP:4 * NP]).then_inc(sel_made, 1)
            dve.wait_ge(sel_made, 1)

            def one_hot(at):
                v.tensor_tensor(oh[:, at.n, :, :], ib[:, at.n, :].unsqueeze(1).to_broadcast([P, TJ, P]),
                                tcol[:, :].unsqueeze(2).to_broadcast([P, TJ, P]), ALU.is_equal).then_inc(oh_made, 1)

            def keep_values(at):
                dve.wait_ge(values_picked, at.n + 1)
                for b in range(2):
                    block = slice(b * K, (b + 1) * K)
                    last = v.tensor_copy(slot_halves[block, at.n, :], ps[block, 6 + at.par, 4 * b:4 * b + 4])
                last.then_inc(values_kept, 1)

            def x_of(at):
                dve.wait_ge(rows_in, 16 * NP)
                v.tensor_scalar(xsel[:, at.n, :], xsel[:, at.n, :], slotval[:, at.n, 0:1], None, ALU.mult).then_inc(x_made, 1)

            def pick_period(at):
                if at.back(-2).below(NP):
                    one_hot(at.back(-2))
                keep_values(at)

            for i in range(4):
                dve.wait_ge(ib_copied, i + 1)
                if i == 0:
                    one_hot(At(0, 0))
                    one_hot(At(0, 1))
            ahead(dve, pick_period)

            dve.wait_ge(values_kept, NP)
            link(v.tensor_tensor(slotval[:, :, :], slot_halves[:, :, 0:2], slot_halves[:, :, 2:4], ALU.add))
            dve.wait_ge(inv_made, HD // 2)
            HF = HD // 2
            link(v.tensor_tensor(ang[:, :].rearrange("p (n d) -> p n d", d=HF), slotval[:, :, 1].unsqueeze(2).to_broadcast([P, NP, HF]),
                                 inv[:, :].unsqueeze(1).to_broadcast([P, NP, HF]), ALU.mult))
            v.tensor_scalar(trn[:, 0, :], ang[:, :], TWO_PI_INV, 0.25, ALU.mult, ALU.add)
            link(v.tensor_scalar(trn[:, 1, :], ang[:, :], TWO_PI_INV, None, ALU.mult))
            link(v.tensor_scalar(trn[:, :, :], trn[:, :, :], MAGIC, MAGIC, ALU.add, ALU.subtract))
            trf = trg[:, :, :, :].rearrange("p a n d -> p a (n d)")
            twice = ang[:, :].unsqueeze(1).to_broadcast([P, 2, NP * HF])
            link(v.scalar_tensor_tensor(trf, trn[:, :, :], -C1, twice, ALU.mult, ALU.add))
            link(v.scalar_tensor_tensor(trf, trn[:, :, :], -C2, trf, ALU.mult, ALU.add))
            link(v.scalar_tensor_tensor(trf, trn[:, :, :], -C3, trf, ALU.mult, ALU.add))
            link(v.tensor_scalar(trf[:, 0, :], trf[:, 0, :], HALF_PI, None, ALU.add))
            v.tensor_scalar(trn[:, :, :], trf, PI, -PI, ALU.min, ALU.max).then_inc(ang_ready, 1)

            def mask_keep(at):
                dve.wait_ge(mask_picked, at.n + 1)
                for b in range(2):
                    block = slice(b * K, (b + 1) * K)
                    last = v.tensor_copy(mall[block, at.n, :], ps[block, 2 + at.par, block])
                last.then_inc(mall_done, 1)

            def slot_period(at):
                x_of(at)
                if at.had(1):
                    mask_keep(at.back(1))

            plain(dve, slot_period)
            mask_keep(At(NP // RING, -1))

            dve.wait_ge(rstd_done, 2)
            dve.wait_ge(mall_done, NP)
            dve.wait_ge(sin_done, 1)

            def normed(at):
                if at.had(2):
                    dve.wait_ge(hn_turned, at.n - 1)
                v.tensor_scalar(hn[at.par], xsel[:, at.n, :], rstd_of(rstd, at), None, ALU.mult).then_inc(hn_made, 1)

            def normed2(at):
                dve.wait_ge(rstd2_done, at.n + 1)
                v.tensor_scalar(hn2[at.par], x1[:, at.n, :], norm2[at.par][:, 2:3], None, ALU.mult).then_inc(hn2_made, 1)

            def softmax_in(at):
                dve.wait_ge(scores_ready, at.n + 1)
                if at.had(1):
                    dve.wait_ge(exp_done, at.n)
                mask = mall[:, at.n, :].unsqueeze(1).unsqueeze(1).to_broadcast([P, 4, 4, K])
                v.tensor_tensor(sc.rearrange("p (t h) k -> p t h k", t=4), ps[:, 0:4, 0:256].rearrange("p t (h k) -> p t h k", k=K),
                                mask, ALU.add).then_inc(s_done, 1)
                dve.wait_ge(s_done, at.n + 1)
                v.tensor_reduce(mx[at.par], sc[:, :, 0:KC], AX.X, ALU.max).then_inc(mx_done, 1)
                dve.wait_ge(mx_done, at.n + 1)
                v.tensor_tensor(sc[:, :, 0:KC], sc[:, :, 0:KC], mx[at.par].unsqueeze(2).to_broadcast([P, H, KC]),
                                ALU.subtract).then_inc(sub_done, 1)

            def rope(at):
                dve.wait_ge(qk_ready, at.n + 1)
                if at.had(2):
                    dve.wait_ge(qk_turned, at.n - 1)
                src = ps[:, 7, :].rearrange("p (h a d) -> p h a d", a=2, d=HF)
                dst = rq[at.par].rearrange("p (h a d) -> p h a d", a=2, d=HF)
                tmp = rtmp.rearrange("p (h a d) -> p h a d", a=2, d=HF)
                cos = trg[:, 0, at.n, :].unsqueeze(1)
                sin = trg[:, 1, at.n, :].unsqueeze(1)
                v.tensor_tensor(dst, src, cos.unsqueeze(1).to_broadcast([P, 2 * H, 2, HF]), ALU.mult)
                for half in range(2):
                    last = v.tensor_tensor(tmp[:, :, half, :], src[:, :, 1 - half, :], sin.to_broadcast([P, 2 * H, HF]), ALU.mult)
                last.then_inc(rope_part, 1)
                dve.wait_ge(rope_part, at.n + 1)
                for half, op in ((0, ALU.subtract), (1, ALU.add)):
                    last = v.tensor_tensor(dst[:, :, half, :], dst[:, :, half, :], tmp[:, :, half, :], op)
                last.then_inc(rope_done, 1)

            def output_of(at):
                dve.wait_ge(pv_ready, at.n + 1)
                o = ps[:, 4, 0:H // 2 * 34].rearrange("p (n d) -> p n d", d=34)
                v.reciprocal(rd[at.par].rearrange("p (n h) -> p n h", h=2), o[:, :, 32:34]).then_inc(rd_done, 1)
                dve.wait_ge(rd_done, at.n + 1)
                if at.had(2):
                    dve.wait_ge(o_turned, at.n - 1)
                v.tensor_tensor(osb[at.par].rearrange("p (n h d) -> p n h d", h=2, d=HD), o[:, :, 0:32].rearrange("p n (h d) -> p n h d", h=2),
                                rd[at.par].rearrange("p (n h) -> p n h", h=2).unsqueeze(3).to_broadcast([P, H // 2, 2, HD]),
                                ALU.mult).then_inc(o_done, 1)

            def residual(at):
                dve.wait_ge(o_projected, at.n + 1)
                v.tensor_tensor(x1[:, at.n, :], ps[:, 6, 0:C], xsel[:, at.n, :], ALU.add).then_inc(x1_done, 1)

            def att_period(at):
                if at.below(NP):
                    rope(at)
                if at.back(-2).below(NP):
                    normed(at.back(-2))
                if at.is_pair(4):
                    normed2(at.back(4))
                if at.is_pair(1):
                    softmax_in(at.back(1))
                if at.is_pair(2):
                    output_of(at.back(2))
                if at.is_pair(3):
                    residual(at.back(3))

            normed(At(0, 0))
            normed(At(0, 1))
            pairs(dve, att_period)

            dve.wait_ge(x1_done, NP)

            def split_h2(g):
                dve.wait_ge(h2T_done, GP * (g.n + 1))
                if g.had(2):
                    dve.wait_ge(up_ready, FC // 2 * (g.n - 1))
                full = h2T[:, :, bass.ts(g.n, GP * P)]
                v.tensor_copy(h2_hi[g.par], full).then_inc(h2_rounded, 1)
                dve.wait_ge(h2_rounded, g.n + 1)
                v.tensor_tensor(h2_lo[g.par], full, h2_hi[g.par].bitcast(fp32), ALU.subtract).then_inc(h2_split, 1)

            def split_u(g):
                dve.wait_ge(gelu_done, FC // 2 * (g.n + 1))
                if g.had(1):
                    dve.wait_ge(down_ready, g.n)
                v.tensor_copy(u_hi, uT[g.par]).then_inc(u_rounded, 1)
                dve.wait_ge(u_rounded, g.n + 1)
                v.tensor_tensor(u_lo, uT[g.par], u_hi.bitcast(fp32), ALU.subtract).then_inc(u_split, 1)

            def mlp_period(g):
                if g.back(-2).below(NG):
                    split_h2(g.back(-2))
                if g.back(-1).below(NG):
                    split_u(g.back(-1))
                finish(g)

            def finish(g):
                x2g, f, pair0 = x2[g.par], fst[:, g.par, :, :], bass.ts(g.n, GP)
                v.tensor_tensor(share[g.par], xsel[:, pair0, :], sel[:, 3, pair0].unsqueeze(2).to_broadcast([P, GP, C]), ALU.mult)
                dve.wait_ge(down_ready, g.n + 1)
                v.tensor_tensor(x2g, ps[:, 4 + g.par, :].rearrange("p (i c) -> p i c", c=C), x1[:, pair0, :], ALU.add).then_inc(x2_read, 1)
                dve.wait_ge(x2_read, g.n + 1)
                v.tensor_tensor(x2g, x2g, sel[:, 2, pair0].unsqueeze(2).to_broadcast([P, GP, C]), ALU.mult).then_inc(x2_weighted, 1)
                dve.wait_ge(x2_weighted, g.n + 1)
                v.tensor_tensor(x2g, x2g, share[g.par], ALU.add).then_inc(x2_done, 1)
                dve.wait_ge(x2_done, g.n + 1)
                for i in range(GP):
                    last = v.bn_stats(f[:, i, 0:6], x2g[:, i, :])
                last.then_inc(x2_bn_done, 1)
                dve.wait_ge(x2_bn_done, g.n + 1)
                v.memset(dtick[:, :], 0.0)
                for i in range(GP):
                    last = v.bn_aggr(f[:, i, 6:8], f[:, i, 0:6])
                last.then_inc(x2_aggr_done, 1)
                dve.wait_ge(x2_aggr_done, g.n + 1)
                v.tensor_scalar(f[:, :, 8], f[:, :, 7], EPS, None, ALU.add).then_inc(x2_var_ready, 1)
                dve.wait_ge(x2_pow_done, g.n + 1)
                for i in range(GP):
                    last = v.tensor_scalar(outr[:, pair_at(g, i), :].rearrange("p a c -> p (a c)"), x2g[:, i, :],
                                           f[:, i, 6:7], f[:, i, 9:10], ALU.subtract, ALU.mult)
                last.then_inc(outr_ready, 1)

            split_h2(At(0, 0, 2))
            split_h2(At(0, 1, 2))
            split_u(At(0, 0, 2))
            by_twos(dve, NG, mlp_period)


def kernel(**inputs):
    import numpy as np
    import concourse.bacc as bacc
    from concourse import mybir as mb
    from concourse.bass_utils import run_bass_kernel_spmd as run

    nc = bacc.Bacc("TRN2", target_bir_lowering=False, num_devices=1)
    x = np.asarray(inputs["L0_attn_x"])
    arrays = {
        "x_tok": x,
        "x_chan": x.transpose(0, 2, 1),
        "w_attn": np.stack([np.asarray(inputs["L0_attn_" + n]).T for n in ("Wk", "Wv", "Wr", "Wo")]),
        "columns": np.concatenate(
            [np.asarray(inputs["L0_" + n]).reshape(-1, 128).T for n in ("attn_spatial_first", "attn_spatial_decay", "ffn_ln1", "ffn_ln2")]
            + [np.asarray(inputs["L0_attn_mix_" + n])[:128, None] for n in "kvr"], axis=1),
        "mask_rows": np.asarray(inputs["L0_ffn_attention_mask"]).reshape(-1, 512),
        "positions": np.asarray(inputs["L0_ffn_position_ids"]).reshape(-1, 1),
        "router_w": np.asarray(inputs["L0_ffn_router_w"]).reshape(-1),
        "router_b": inputs["L0_ffn_router_b"],
        "w_qk": np.concatenate([inputs["L0_ffn_wq"], inputs["L0_ffn_wk"]], axis=1),
        "w_v": inputs["L0_ffn_wv"],
        "w_o": inputs["L0_ffn_wo"],
        "w_up": inputs["L0_ffn_w1"],
        "w_down": inputs["L0_ffn_w2"],
    }
    arrays = {n: np.ascontiguousarray(a) for n, a in arrays.items()}
    aps = [nc.dram_tensor(n, a.shape, mb.dt.from_np(a.dtype), kind="ExternalInput").ap() for n, a in arrays.items()]
    out = nc.dram_tensor("out", x.shape, mb.dt.float32, kind="ExternalOutput").ap()
    rwkv_then_selected_block_kernel(nc, *aps, out)
    return run(nc, [arrays], core_ids=[0]).results[0]["out"]
```
